# Optimizing a Trainium2 kernel written in Bass

```python
import numpy as np
import jax
import jax.numpy as jnp

def _softmax(x, axis=-1):
    return jax.nn.softmax(x, axis=axis)

def _gelu(x):
    return jax.nn.gelu(x, approximate=True)

def _silu(x):
    return jax.nn.silu(x)

def _sigmoid(x):
    return jax.nn.sigmoid(x)

def _layernorm(x, axis=-1, eps=1e-05):
    m = jnp.mean(x, axis=axis, keepdims=True)
    v = jnp.var(x, axis=axis, keepdims=True)
    return (x - m) / jnp.sqrt(v + eps)

def _scatter_add(tgt, idx, src, axis=0):
    return tgt.at[idx].add(src)

def _segment_sum(src, seg, n):
    return jax.ops.segment_sum(src, seg, n)
kernel_name = 'mk_cond_resid_d4_seqx_r4_c0a7e5'

def setup_inputs(seed: int=0):
    np.random.seed(seed)
    _w = jnp.asarray

    def _rec_inputs():
        import jax
        import jax.numpy as jnp
        _rk = jax.random.key(seed)
        x = -0.000125 + 0.9999 * jax.random.normal(jax.random.fold_in(_rk, 1), (32, 64, 1024), jnp.float32)
        _lenS = 64 - jax.random.randint(jax.random.fold_in(_rk, 7), (32,), 0, max(1, 64 // 4) + 1, jnp.int32)
        _lenS2 = 64 - jax.random.randint(jax.random.fold_in(_rk, 8), (32,), 0, max(1, 64 // 4) + 1, jnp.int32)
        itok_B_0_23 = jax.random.randint(jax.random.fold_in(_rk, 11), (32,), 0, 24, jnp.int32)
        itok_B_0_7 = jax.random.randint(jax.random.fold_in(_rk, 12), (32,), 0, 8, jnp.int32)
        itok_B_0_31 = jax.random.randint(jax.random.fold_in(_rk, 13), (32,), 0, 32, jnp.int32)
        condB_scale = 0.000342416 + 0.0128191 * jax.random.normal(jax.random.fold_in(_rk, 14), (32,), jnp.float32)
        itok_Bx4096x4096_0_255 = jax.random.randint(jax.random.fold_in(_rk, 15), (32, 1024, 1024), 0, 64, jnp.int32)
        condB_wscale = jax.random.uniform(jax.random.fold_in(_rk, 16), (32,), jnp.float32, 0.0, 0.00091742)
        itok_Bx4096_0_255 = jax.random.randint(jax.random.fold_in(_rk, 18), (32, 1024), 0, 64, jnp.int32)
        condB_bscale = jax.random.uniform(jax.random.fold_in(_rk, 19), (32,), jnp.float32, 0.0, 0.000800939)
        return (x, itok_B_0_23, itok_B_0_7, itok_B_0_31, condB_scale, itok_Bx4096x4096_0_255, condB_wscale, itok_Bx4096_0_255, condB_bscale, _lenS)
    x, itok_B_0_23, itok_B_0_7, itok_B_0_31, condB_scale, itok_Bx4096x4096_0_255, condB_wscale, itok_Bx4096_0_255, condB_bscale, _lenS = _rec_inputs()

    def _L0_cond_setup():
        import jax, jax.numpy as jnp
        import numpy as np
        R = 16
        ALPHA = 32
        SCALING = ALPHA / R
        SLOTS = 32
        IN_F = 1024
        OUT_F = 1024
        B, T = (8, 256)
        key = jax.random.key(seed)
        k1, k2, k3, k4, k5, k6 = jax.random.split(key, 6)
        x = jax.random.normal(k1, (B, T, IN_F), dtype=jnp.float32)
        adapter_mapping = jax.random.randint(k2, (B,), 0, SLOTS, dtype=jnp.int32)
        W = jax.random.normal(k3, (OUT_F, IN_F), dtype=jnp.float32) * 0.02
        b = jax.random.normal(k4, (OUT_F,), dtype=jnp.float32) * 0.02
        lora_As = jax.random.normal(k5, (SLOTS, IN_F, R), dtype=jnp.float32) * 0.02
        lora_Bs = jax.random.normal(k6, (SLOTS, R, OUT_F), dtype=jnp.float32) * 0.02
        return {'x': x, 'adapter_mapping': adapter_mapping, 'W': W, 'b': b, 'lora_As': lora_As, 'lora_Bs': lora_Bs}
    _L0_cond_all = _L0_cond_setup()
    _L0_cond_in = {k: v for k, v in _L0_cond_all.items() if k in ('W', 'b', 'lora_As', 'lora_Bs')}
    del _L0_cond_all

    def _L1_cond_setup():
        import jax, jax.numpy as jnp
        import numpy as np
        TOP_K = 2
        LANG_BIAS = 5.0
        SCALING = 32.0 / 16.0
        LANGUAGE_PAD_ID = -1
        key = jax.random.key(seed)
        ks = jax.random.split(key, 6)
        B, T, D, O, E, R = (4, 512, 1024, 1024, 8, 16)
        x = jax.random.normal(ks[0], (B, T, D), dtype=jnp.float32)
        language_ids = jax.random.randint(ks[1], (B,), 0, E).astype(jnp.int64)
        W = jax.random.normal(ks[2], (O, D), dtype=jnp.float32) * (1.0 / np.sqrt(D))
        Wr = jax.random.normal(ks[3], (E, D), dtype=jnp.float32) * (1.0 / np.sqrt(D))
        A = jax.random.normal(ks[4], (E, R, D), dtype=jnp.float32) * (1.0 / np.sqrt(D))
        Bm = jax.random.normal(ks[5], (O, R), dtype=jnp.float32) * 0.0
        Bm = jnp.broadcast_to(Bm, (E, O, R)) + jax.random.normal(ks[5], (E, O, R), dtype=jnp.float32) * 0.02
        return {'x': x, 'language_ids': language_ids, 'W': W, 'Wr': Wr, 'A': A, 'B': Bm}
    _L1_cond_all = _L1_cond_setup()
    _L1_cond_in = {k: v for k, v in _L1_cond_all.items() if k in ('W', 'Wr', 'A', 'B')}
    del _L1_cond_all

    def _L2_cond_setup():
        import jax, jax.numpy as jnp
        import numpy as np
        S, C, D = (32, 64, 64)
        B, T = (64, 1024)
        key = jax.random.key(seed)
        k_x, k_w, k_s = jax.random.split(key, 3)
        x = jax.random.normal(k_x, (B, C, T), dtype=jnp.float32)
        subjects = jax.random.randint(k_s, (B,), 0, S, dtype=jnp.int64)
        std = float(np.sqrt(2.0 / (C + D)))
        weights = jax.random.normal(k_w, (S, C, D), dtype=jnp.float32) * std * (1.0 / np.sqrt(C))
        biases = jnp.zeros((S, 1, D), dtype=jnp.float32)
        return {'x': x, 'subjects': subjects, 'weights': weights, 'biases': biases}
    _L2_cond_all = _L2_cond_setup()
    _L2_cond_in = {k: v for k, v in _L2_cond_all.items() if k in ('weights', 'biases')}
    del _L2_cond_all

    def _L3_cond_setup():
        import jax, jax.numpy as jnp
        import numpy as np
        key = jax.random.key(seed)
        ks = jax.random.split(key, 10)
        N, OUT, IN = (8, 1024, 1024)
        B, S = (8, 512)
        return {'x': jax.random.normal(ks[0], (B, S, IN), dtype=jnp.float32), 'weight': jax.random.normal(ks[1], (OUT, IN), dtype=jnp.float32) * 0.02, 'bias': jax.random.normal(ks[2], (OUT,), dtype=jnp.float32) * 0.02, 'scale': jax.random.normal(ks[3], (N,), dtype=jnp.float32) * 0.01, 'wq': jax.random.randint(ks[4], (N, OUT, IN), 0, 64, dtype=jnp.int32), 'wscale': jax.random.uniform(ks[5], (N,), dtype=jnp.float32) * 0.001, 'wzp': jax.random.randint(ks[6], (N,), 0, 64, dtype=jnp.int32), 'bq': jax.random.randint(ks[7], (N, OUT), 0, 64, dtype=jnp.int32), 'bscale': jax.random.uniform(ks[8], (N,), dtype=jnp.float32) * 0.001, 'bzp': jax.random.randint(ks[9], (N,), 0, 64, dtype=jnp.int32)}
    _L3_cond_all = _L3_cond_setup()
    _L3_cond_in = {k: v for k, v in _L3_cond_all.items() if k in ('weight', 'bias')}
    del _L3_cond_all
    return {'x': x, 'itok_B_0_23': itok_B_0_23, 'itok_B_0_7': itok_B_0_7, 'itok_B_0_31': itok_B_0_31, 'condB_scale': condB_scale, 'itok_Bx4096x4096_0_255': itok_Bx4096x4096_0_255, 'condB_wscale': condB_wscale, 'itok_Bx4096_0_255': itok_Bx4096_0_255, 'condB_bscale': condB_bscale, '_lenS': _lenS, 'L0_cond_W': _L0_cond_in['W'], 'L0_cond_b': _L0_cond_in['b'], 'L0_cond_lora_As': _L0_cond_in['lora_As'], 'L0_cond_lora_Bs': _L0_cond_in['lora_Bs'], 'L1_cond_W': _L1_cond_in['W'], 'L1_cond_Wr': _L1_cond_in['Wr'], 'L1_cond_A': _L1_cond_in['A'], 'L1_cond_B': _L1_cond_in['B'], 'L2_cond_weights': _L2_cond_in['weights'], 'L2_cond_biases': _L2_cond_in['biases'], 'L3_cond_weight': _L3_cond_in['weight'], 'L3_cond_bias': _L3_cond_in['bias']}

def reference(x, itok_B_0_23, itok_B_0_7, itok_B_0_31, condB_scale, itok_Bx4096x4096_0_255, condB_wscale, itok_Bx4096_0_255, condB_bscale, _lenS, L0_cond_W, L0_cond_b, L0_cond_lora_As, L0_cond_lora_Bs, L1_cond_W, L1_cond_Wr, L1_cond_A, L1_cond_B, L2_cond_weights, L2_cond_biases, L3_cond_weight, L3_cond_bias):
    import jax
    import jax.numpy as jnp

    def _L0_cond_ref(x, adapter_mapping, W, b, lora_As, lora_Bs):
        import jax, jax.numpy as jnp
        import numpy as np
        R = 16
        ALPHA = 32
        SCALING = ALPHA / R
        SLOTS = 32
        IN_F = 1024
        OUT_F = 1024
        B, T = (8, 256)
        base_out = jnp.einsum('bti,oi->bto', x, W) + b
        A = lora_As[adapter_mapping]
        Bm = lora_Bs[adapter_mapping]
        lora_h = jnp.einsum('bti,bir->btr', x, A)
        lora_out = jnp.einsum('btr,bro->bto', lora_h, Bm)
        return base_out + lora_out * SCALING

    def _L1_cond_ref(x, language_ids, W, Wr, A, B):
        import jax, jax.numpy as jnp
        import numpy as np
        TOP_K = 2
        LANG_BIAS = 5.0
        SCALING = 32.0 / 16.0
        LANGUAGE_PAD_ID = -1
        base = jnp.einsum('btd,od->bto', x, W)
        E = Wr.shape[0]
        logits = jnp.einsum('btd,ed->bte', x.astype(jnp.float32), Wr.astype(jnp.float32))
        expert_targets = language_ids
        valid = expert_targets >= 0
        tgt = jnp.where(valid, expert_targets, 0)
        bias = jax.nn.one_hot(tgt, E, dtype=logits.dtype) * LANG_BIAS
        bias = jnp.where(valid[:, None], bias, 0.0)
        logits = logits + bias[:, None, :]
        topw, topi = jax.lax.top_k(logits, TOP_K)
        weights = jax.nn.softmax(topw, axis=-1)
        gates = jnp.sum(jax.nn.one_hot(topi, E, dtype=weights.dtype) * weights[..., None], axis=-2)
        gates = gates.astype(x.dtype)
        h = jnp.einsum('btd,erd->bter', x, A)
        lora_out = jnp.einsum('bter,bte,eor->bto', h, gates, B)
        return base + SCALING * lora_out

    def _L2_cond_ref(x, subjects, weights, biases):
        import jax, jax.numpy as jnp
        import numpy as np
        S, C, D = (32, 64, 64)
        B, T = (64, 1024)
        w = weights[subjects]
        b = biases[subjects]
        out = jnp.einsum('bct,bcd->bdt', x, w)
        return out + jnp.transpose(b, (0, 2, 1))

    def _L3_cond_ref(x, weight, bias, scale, wq, wscale, wzp, bq, bscale, bzp):
        import jax, jax.numpy as jnp
        import numpy as np
        f32 = jnp.float32
        dW = jnp.einsum('i,ijk->jk', scale * wscale, wq.astype(f32)) + jnp.dot(scale, wzp.astype(f32))
        W = weight + dW
        db = jnp.einsum('i,ij->j', scale * bscale, bq.astype(f32)) + jnp.dot(scale, bzp.astype(f32))
        b = bias + db
        return jnp.einsum('bsi,oi->bso', x, W) + b
    x = x + _L0_cond_ref(x, itok_B_0_23, L0_cond_W, L0_cond_b, L0_cond_lora_As, L0_cond_lora_Bs)
    x = x + _L1_cond_ref(x, itok_B_0_7, L1_cond_W, L1_cond_Wr, L1_cond_A, L1_cond_B)
    x = x + _L2_cond_ref(x, itok_B_0_31, L2_cond_weights, L2_cond_biases)
    x = x + _L3_cond_ref(x, L3_cond_weight, L3_cond_bias, condB_scale, itok_Bx4096x4096_0_255, condB_wscale, _lenS, itok_Bx4096_0_255, condB_bscale, _lenS)
    return x

_drawn_inputs = setup_inputs


def setup_inputs(seed=0):
    import zlib

    import numpy as np

    out = dict(_drawn_inputs(seed))
    spreads = {'L2_cond_biases': (0.0, 0.1)}
    factors = {'condB_wscale': 64.0,
     'condB_bscale': 64.0,
     'L0_cond_b': 8.0,
     'L1_cond_Wr': 7.153,
     'L3_cond_weight': 8.0,
     'L3_cond_bias': 64.0}
    for name, (base, spread) in spreads.items():
        noise = np.random.default_rng([zlib.crc32(name.encode()), seed]).standard_normal(out[name].shape)
        drawn = base * np.exp(spread * noise) if base else spread * noise
        out[name] = jnp.asarray(drawn.astype(out[name].dtype))
    for name, factor in factors.items():
        out[name] = (out[name] * factor).astype(out[name].dtype)
    return out
```

```python
from contextlib import ExitStack

import concourse.bass as bass
from concourse import mybir

F32 = mybir.dt.float32
F32R = mybir.dt.float32r
I32 = mybir.dt.int32
U32 = mybir.dt.uint32
ALU = mybir.AluOpType
ACT = mybir.ActivationFunctionType
AX_X = mybir.AxisListType.X
ds = bass.ds

P = 128
BATCH, SEQ, D = 32, 64, 1024
T = BATCH * SEQ
KT = D // P
TT = T // P
GT = 256
NG = T // GT
GB = GT // SEQ
R = 16
NE = 8
ER = NE * R
AW = ER + NE
NB = 512
NQ = 32
HB = 4
HALF = HB * P
RING = 4
L0_Q = NQ * HB
L1_QT = 6
L3_QT = 2
LANG_BIAS = 5.0
SCALING = 2.0
assert L0_Q == NG * 16 and TT * (L1_QT + L3_QT) == NQ * HB


def program(nc, x, scale, wscale, bscale, len_s, slot_id, lang_id, subj_id, wq, bq,
            W0, b0, lora_A, lora_B, W1, Wr, A1, B1, w2, bias2, W3, b3, y):
    w3_upper = nc.dram_tensor("w3_upper", (HALF, D), F32, kind="Internal").ap()
    x_rows = x.rearrange("b s d -> (b s) d")
    y_rows = y.rearrange("b s d -> (b s) d")
    lora_A_v = lora_A.rearrange("s (p k) r -> s p (k r)", k=KT)
    row = lambda v: v.rearrange("(a n) -> a n", a=1)

    with ExitStack() as ctx:
        def sb(name, shape, dt=F32, where=ctx):
            return where.enter_context(nc.sbuf_tensor(name, shape, dt))

        def sem(name):
            return ctx.enter_context(nc.semaphore(name))

        ident = sb("ident", [P, P])
        w_hi = sb("w_hi", [P, KT, D], F32R)
        w_lo = sb("w_lo", [P, KT, D], F32R)
        act = sb("act", [P, KT, T])
        w3_sum = sb("w3_sum", [P, HB, D])
        ring = sb("ring", [P, RING, D], I32)
        coef = sb("coef", [P, NQ])
        s0 = sb("s0", [P, 1])
        b0_col = sb("b0_col", [P, KT])
        lang_bias = sb("lang_bias", [P, TT, NE])
        iota8 = sb("iota8", [P, NE])
        subj_row = sb("subj_row", [1, BATCH], I32)
        slot_row = sb("slot_row", [1, BATCH], I32)
        own = sb("own", [P, GB, 1])
        ps = ctx.enter_context(nc.psum_tensor("ps", [P, 8, NB], F32))

        def banks(b):
            return ps[:, b:b + 2, :].rearrange("p b n -> p (b n)")

        def tiles(b):
            return ps[:, b:b + 2, :].rearrange("p b (k n) -> p (b k) n", n=P)

        ring_ld = [sem(f"ring_ld{s}") for s in range(RING)]
        sum_done = sem("sum_done")
        y_out = sem("y_out")
        x2_lo_d = sem("x2_lo_d")
        x3_out = sem("x3_out")
        y3_out_sems = [sem(f"y3_out_{h}") for h in ("up", "low")]
        prep_lo = [sem(f"prep_lo{n}") for n in range(3)]
        base_mm = sem("base_mm")
        free_two = [y_out, x2_lo_d, *y3_out_sems, *prep_lo]
        free_one = [x3_out, base_mm]
        dma_w3 = sem("dma_w3")

        def load_q(eng, block, expert, half):
            r0 = half * HALF + block * P
            eng.dma_start(ring[:, block, :], wq[ds(expert, 1), r0:r0 + P, :]
                          .rearrange("a p n -> p (a n)")).then_inc(ring_ld[block], 16)

        def stream_q(eng, it, per, n0, js, half):
            for j in js:
                eng.wait_ge(sum_done, it * per + (n0 + j + RING + 1))
                load_q(eng, j % RING, it * (per // RING) + (n0 - half * L0_Q + j + RING) // RING, half)

        def add_q(it, per, n0, js, half):
            for j in js:
                s = j % RING
                nc.vector.wait_ge(ring_ld[s], it * (4 * per) + 16 * ((n0 + j) // RING + 1))
                nc.vector.wait_ge(sum_done, it * per + (n0 + j + 1))
                expert = it * (per // RING) + (n0 - half * L0_Q + j) // RING
                nc.vector.scalar_tensor_tensor(
                    out=w3_sum[:, s, :], in0=ring[:, s, :], scalar=coef[:, ds(expert, 1)],
                    in1=w3_sum[:, s, :], op0=ALU.mult, op1=ALU.add).then_inc(sum_done, 1)

        class Prep:

            def __init__(self, name, w, st, blocks, strided, lo):
                self.w, self.st, self.n, self.strided = w, st, blocks, strided
                self.st_ld = [sem(f"{name}_ld{d}") for d in range(2)]
                self.st_id = sem(f"{name}_id")
                self.tp = sem(f"{name}_tp")
                self.hi = sem(f"{name}_hi")
                self.lo = lo

            def sync(self, eng):
                def load(it, d):
                    eng.dma_start(self.st[:, d, :], self.w[ds(it * 2 * P + d * P, P), :])\
                       .then_inc(self.st_ld[d], 16)
                for d in range(2):
                    load(0, d)
                with eng.Fori(1, self.n // 2) as it:
                    for d in range(2):
                        eng.wait_ge(self.tp, it * 2 + (d - 1))
                        load(it, d)

            def pool(self, eng):
                with eng.Fori(0, self.n // 2) as it:
                    for d in range(2):
                        eng.wait_ge(self.st_ld[d], it * 16 + 16)
                        diag = self.st[:, d, ds(it * 2 * P + d * P, P)]
                        nc.gpsimd.tensor_tensor(diag, diag, ident[:], ALU.add).then_inc(self.st_id, 1)

            def tensor(self, eng):
                with eng.Fori(0, self.n // 2) as it:
                    for d in range(2):
                        eng.wait_ge(self.st_id, it * 2 + (d + 1))
                        eng.wait_ge(self.lo, it * 2 + (d + 1))
                        for k in range(KT):
                            src = self.st[:, d, k::KT] if self.strided else self.st[:, d, k * P:(k + 1) * P]
                            last = nc.tensor.transpose(banks(2 * d)[:, k * P:(k + 1) * P], src, ident[:])
                        last.then_inc(self.tp, 1)

            def scalar(self, eng):
                with eng.Fori(0, self.n // 2) as it:
                    for d in range(2):
                        eng.wait_ge(self.tp, it * 2 + (d + 1))
                        nc.scalar.activation(w_hi[:, :, ds(it * 2 * P + d * P, P)], tiles(2 * d), ACT.Copy)\
                          .then_inc(self.hi, 1)

            def vector(self, eng):
                with eng.Fori(0, self.n // 2) as it:
                    for d in range(2):
                        eng.wait_ge(self.hi, it * 2 + (d + 1))
                        o = ds(it * 2 * P + d * P, P)
                        nc.vector.tensor_tensor(w_lo[:, :, o], tiles(2 * d), w_hi[:, :, o].bitcast(F32),
                                                ALU.subtract).then_inc(self.lo, 1)

        with ExitStack() as ph:
            st = sb("st_w0", [P, 2, D], F32, ph)
            scale_bc = sb("scale_bc", [P, NQ], F32, ph)
            wscale_bc = sb("wscale_bc", [P, NQ], F32, ph)
            len_bc = sb("len_bc", [P, NQ], I32, ph)
            len_f = sb("len_f", [P, NQ], F32, ph)
            lang_bc = sb("lang_bc", [P, BATCH], I32, ph)
            lang_tt = sb("lang_tt", [P, TT, 1], F32, ph)
            same = sb("same", [P, 2 * GB], F32, ph)
            consts_ld = sem("consts_ld")
            rows_ld = sem("rows_ld")
            cst = sem("cst")
            dve_s = sem("dve_s")
            prep0 = Prep("w0", W0, st, KT, True, prep_lo[0])
            block = ph.enter_context(nc.Block())

            @block.sync
            def _(sp):
                prep0.sync(sp)
                for b in range(HB):
                    load_q(sp, b, 0, 0)
                sp.dma_start(w3_sum[:], W3[0:HALF, :].rearrange("(b p) n -> p b n", p=P)).then_inc(dma_w3, 16)

            @block.gpsimd
            def _(pool):
                nc.gpsimd.memset(ident[:], 0.0).then_inc(cst, 1)
                pool.wait_ge(cst, 1)
                nc.gpsimd.affine_select(out=ident[:], in_=ident[:], compare_op=ALU.not_equal, fill=1.0, base=0,
                                        pattern=[[-1, P]], channel_multiplier=1).then_inc(cst, 1)
                pool.sem_inc(sum_done, RING)
                for s in free_two:
                    pool.sem_inc(s, 2)
                for s in free_one:
                    pool.sem_inc(s, 1)
                pool.wait_ge(cst, 2)
                prep0.pool(pool)
                nc.gpsimd.iota(iota8[:], pattern=[[1, NE]], base=0, channel_multiplier=0,
                               allow_small_or_imprecise_dtypes=True).then_inc(cst, 1)
                nc.gpsimd.memset(same[:], SCALING).then_inc(cst, 1)
                pool.wait_ge(cst, 4)
                nc.gpsimd.affine_select(out=same[:], in_=same[:], compare_op=ALU.is_ge, fill=0.0, base=0,
                                        pattern=[[-R, 2 * GB]], channel_multiplier=1).then_inc(cst, 1)
                pool.wait_ge(cst, 5)
                nc.gpsimd.affine_select(out=same[:], in_=same[:], compare_op=ALU.is_ge, fill=0.0, base=R - 1,
                                        pattern=[[R, 2 * GB]], channel_multiplier=-1).then_inc(cst, 1)
                pool.wait_ge(cst, 6)
                nc.gpsimd.tensor_tensor(own[:, :, 0], same[:, 0:GB], same[:, GB:2 * GB], ALU.add).then_inc(cst, 1)

            @block.scalar
            def _(act_e):
                for dst, src in ((scale_bc, scale), (wscale_bc, wscale), (len_bc, len_s), (lang_bc, lang_id)):
                    act_e.dma_start(dst[:], row(src).to_broadcast([P, NQ])).then_inc(consts_ld, 16)
                act_e.dma_start(slot_row[:], row(slot_id)).then_inc(rows_ld, 16)
                act_e.dma_start(subj_row[:], row(subj_id)).then_inc(rows_ld, 16)
                with nc.allow_non_contiguous_dma(reason="1024 values of the bias, once"):
                    act_e.dma_start(b0_col[:], b0.rearrange("(k p) -> p k", p=P)).then_inc(rows_ld, 16)
                prep0.scalar(act_e)

            @block.tensor
            def _(pe):
                pe.wait_ge(cst, 2)
                prep0.tensor(pe)

            @block.vector
            def _(dve):
                dve.wait_ge(consts_ld, 64)
                nc.vector.tensor_tensor(coef[:], scale_bc[:], wscale_bc[:], ALU.mult).then_inc(dve_s, 1)
                nc.vector.tensor_copy(len_f[:], len_bc[:]).then_inc(dve_s, 1)
                half = P // 2
                nc.vector.tensor_copy(lang_tt[0:half, :, 0], lang_bc[0:half, 0::2]).then_inc(dve_s, 1)
                nc.vector.tensor_copy(lang_tt[half:P, :, 0], lang_bc[half:P, 1::2]).then_inc(dve_s, 1)
                dve.wait_ge(dve_s, 4)
                nc.vector.tensor_tensor(len_f[:], len_f[:], scale_bc[:], ALU.mult).then_inc(dve_s, 1)
                dve.wait_ge(dve_s, 5)
                nc.vector.reduce_sum(s0[:], len_f[:], AX_X).then_inc(dve_s, 1)
                prep0.vector(dve)
                dve.wait_ge(cst, 3)
                nc.vector.tensor_tensor(lang_bias[:], lang_tt[:].to_broadcast([P, TT, NE]),
                                        iota8[:].rearrange("p (a e) -> p a e", a=1).to_broadcast([P, TT, NE]),
                                        ALU.is_equal).then_inc(dve_s, 1)
                dve.wait_ge(dve_s, 7)
                nc.vector.tensor_scalar(lang_bias[:], lang_bias[:], LANG_BIAS, None, ALU.mult).then_inc(dve_s, 1)
                dve.wait_ge(dma_w3, 16)
                nc.vector.tensor_scalar(w3_sum[:], w3_sum[:], s0[:, 0:1], None, ALU.add).then_inc(dve_s, 1)
                dve.wait_ge(dve_s, 9)

        with ExitStack() as ph:
            x_in = sb("x_in", [P, 2, D], F32, ph)
            xT_hi = sb("xT_hi", [P, KT, GT], F32R, ph)
            xT_lo = sb("xT_lo", [P, KT, GT], F32R, ph)
            A_raw = sb("A_raw", [P, GB, KT * R], F32, ph)
            A_hi = sb("A_hi", [P, KT, P], F32R, ph)
            A_lo = sb("A_lo", [P, KT, P], F32R, ph)
            B_raw = sb("B_raw", [P, D], F32, ph)
            B_st = sb("B_st", [P, D], F32R, ph)
            h_own = sb("h_own", [P, GB, SEQ], F32, ph)
            h_hi = sb("h_hi", [P, GT], F32R, ph)
            h_lo = sb("h_lo", [P, GT], F32R, ph)
            PAIRS = KT // 2
            Y0, HBANK = 4, 6
            x_ld = [sem(f"x_ld{d}") for d in range(2)]
            A_ld, B_ld = sem("A_ld"), sem("B_ld")
            A_hi_d, A_lo_d, B_hi_d, B_lo_d = sem("A_hi_d"), sem("A_lo_d"), sem("B_hi_d"), sem("B_lo_d")
            xtp = sem("xtp")
            xhi_d, xlo_d = sem("xhi_d"), sem("xlo_d")
            x_used = sem("x_used")
            h_mm, h_own_d, h_hi_d, h_lo_d = sem("h_mm"), sem("h_own_d"), sem("h_hi_d"), sem("h_lo_d")
            y_mm = sem("y_mm")
            block = ph.enter_context(nc.Block())

            @block.sync
            def _(sp):
                with sp.Fori(0, NG - 1) as g:
                    stream_q(sp, g, 16, 0, range(16), 0)
                stream_q(sp, NG - 1, 16, 0, range(12), 0)
                stream_q(sp, NG - 1, 16, 0, range(12, 16), 1)

            @block.gpsimd
            def _(pool):
                def load_x(g):
                    for d in range(2):
                        pool.dma_start(x_in[:, d, :], x_rows[ds(g * GT + d * P, P), :]).then_inc(x_ld[d], 16)

                def load_adapters(g):
                    for b in range(GB):
                        s = pool.value_load(slot_row[0:1, ds(g * GB + b, 1)], min_val=0, max_val=lora_A.shape[0] - 1)
                        pool.dma_start(A_raw[:, b, :], lora_A_v[ds(s, 1), :, :].rearrange("a p n -> p (a n)"))\
                            .then_inc(A_ld, 16)
                        for copy in range(2):
                            r0 = copy * GB * R + b * R
                            pool.dma_start(B_raw[r0:r0 + R, :], lora_B[ds(s, 1), :, :].rearrange("a r n -> (a r) n"))\
                                .then_inc(B_ld, 16)

                def split_A(g):
                    pool.wait_ge(A_hi_d, g + 1)
                    raw = A_raw[:].rearrange("p b (k r) -> p k b r", k=KT)
                    for copy in range(2):
                        cols = slice(copy * GB * R, (copy + 1) * GB * R)
                        hi = A_hi[:, :, cols].bitcast(F32).rearrange("p k (b r) -> p k b r", b=GB)
                        lo = A_lo[:, :, cols].rearrange("p k (b r) -> p k b r", b=GB)
                        last = nc.gpsimd.tensor_tensor(lo, raw, hi, ALU.subtract)
                    last.then_inc(A_lo_d, 1)

                def split_B(g):
                    pool.wait_ge(A_lo_d, g + 1)
                    pool.wait_ge(B_hi_d, g + 1)
                    low = slice(GB * R, P)
                    nc.gpsimd.tensor_tensor(B_st[low, :], B_raw[low, :], B_st[low, :].bitcast(F32),
                                            ALU.subtract).then_inc(B_lo_d, 1)

                def group(g):
                    pool.wait_ge(xtp, g * PAIRS + PAIRS)
                    load_x(g + 1)
                    pool.wait_ge(A_lo_d, g + 1)
                    pool.wait_ge(B_lo_d, g + 1)
                    load_adapters(g + 1)
                    split_A(g + 1)
                    split_B(g + 1)

                load_x(0)
                pool.wait_ge(rows_ld, 48)
                load_adapters(0)
                split_A(0)
                split_B(0)
                with pool.Fori(0, NG - 1) as g:
                    group(g)

            @block.scalar
            def _(act_e):
                def split_A(g):
                    act_e.wait_ge(A_ld, g * (16 * GB) + 16 * GB)
                    raw = A_raw[:].rearrange("p b (k r) -> p k b r", k=KT)
                    for copy in range(2):
                        cols = slice(copy * GB * R, (copy + 1) * GB * R)
                        last = nc.scalar.activation(A_hi[:, :, cols].rearrange("p k (b r) -> p k b r", b=GB),
                                                    raw, ACT.Copy)
                    last.then_inc(A_hi_d, 1)

                def split_B(g):
                    act_e.wait_ge(B_ld, g * (32 * GB) + 32 * GB)
                    nc.scalar.activation(B_st[:], B_raw[:], ACT.Copy).then_inc(B_hi_d, 1)

                def split_x(g):
                    for j in range(PAIRS):
                        act_e.wait_ge(xtp, g * PAIRS + (j + 1))
                        if not (isinstance(g, int) and g == 0):
                            act_e.wait_ge(x_used, (g - 1) * PAIRS + (j + 1))
                        nc.scalar.activation(xT_hi[:, 2 * j:2 * j + 2, :].rearrange("p k t -> p (k t)"),
                                             ps[:, j, :], ACT.Copy).then_inc(xhi_d, 1)

                def out(g, o):
                    act_e.wait_ge(y_mm, g * KT + (o + 1))
                    nc.scalar.activation(act[:, o, ds(g * GT, GT)], ps[:, Y0 + o % 2, 0:GT], ACT.Identity,
                                         bias=b0_col[:, o:o + 1]).then_inc(y_out, 1)

                def group(g, more):
                    act_e.wait_ge(h_own_d, g + 1)
                    nc.scalar.activation(h_hi[:], h_own[:].rearrange("p b s -> p (b s)"), ACT.Copy)\
                      .then_inc(h_hi_d, 1)
                    for o in range(3):
                        out(g, o)
                    if more:
                        split_A(g + 1)
                    for o in range(3, KT - 1):
                        out(g, o)
                    if more:
                        split_x(g + 1)
                    out(g, KT - 1)
                    if more:
                        split_B(g + 1)

                act_e.wait_ge(rows_ld, 48)
                split_x(0)
                split_A(0)
                split_B(0)
                with act_e.Fori(0, NG - 1) as g:
                    group(g, True)
                group(NG - 1, False)

            @block.tensor
            def _(pe):
                def transpose_x(g):
                    for d in range(2):
                        pe.wait_ge(x_ld[d], g * 16 + 16)
                    for j in range(PAIRS):
                        for k in (2 * j, 2 * j + 1):
                            for d in range(2):
                                c = (k % 2) * GT + d * P
                                last = nc.tensor.transpose(ps[:, j, c:c + P], x_in[:, d, k::KT], ident[:])
                        last.then_inc(xtp, 1)

                def group(g, more):
                    pe.wait_ge(A_lo_d, g + 1)
                    for k in range(KT):
                        if k % 2 == 0:
                            pe.wait_ge(xlo_d, g * PAIRS + (k // 2 + 1))
                        for n, (a, b) in enumerate(((A_hi, xT_hi), (A_lo, xT_hi), (A_hi, xT_lo))):
                            last = nc.tensor.matmul(ps[:, HBANK, 0:GT], a[:, k, :], b[:, k, :],
                                                    start=(k == 0 and n == 0), stop=(k == KT - 1 and n == 2))
                    last.then_inc(h_mm, 1)

                    def base(o):
                        pe.wait_ge(y_out, g * KT + (o + 1))
                        cols = slice(o * P, (o + 1) * P)
                        for k in range(KT):
                            for n, (a, b) in enumerate(((w_hi, xT_hi), (w_lo, xT_hi), (w_hi, xT_lo))):
                                last = nc.tensor.matmul(ps[:, Y0 + o % 2, 0:GT], a[:, k, cols], b[:, k, :],
                                                        start=(k == 0 and n == 0), stop=False)
                            if o == KT - 1 and k % 2:
                                last.then_inc(x_used, 1)

                    def lora(o):
                        cols = slice(o * P, (o + 1) * P)
                        nc.tensor.matmul(ps[:, Y0 + o % 2, 0:GT], B_st[:, cols], h_hi[:], start=False, stop=False)
                        nc.tensor.matmul(ps[:, Y0 + o % 2, 0:GT], B_st[:, cols], h_lo[:], start=False, stop=True)\
                          .then_inc(y_mm, 1)

                    base(0)
                    base(1)
                    pe.wait_ge(h_lo_d, g + 1)
                    pe.wait_ge(B_lo_d, g + 1)
                    lora(0)
                    lora(1)
                    for o in range(2, KT):
                        base(o)
                        lora(o)
                        if o == 4 and more:
                            transpose_x(g + 1)

                transpose_x(0)
                with pe.Fori(0, NG - 1) as g:
                    group(g, True)
                group(NG - 1, False)

            @block.vector
            def _(dve):
                def split_x(g):
                    for j in range(PAIRS):
                        dve.wait_ge(xhi_d, g * PAIRS + (j + 1))
                        pair = slice(2 * j, 2 * j + 2)
                        nc.vector.tensor_tensor(xT_lo[:, pair, :].rearrange("p k t -> p (k t)"), ps[:, j, :],
                                                xT_hi[:, pair, :].bitcast(F32).rearrange("p k t -> p (k t)"),
                                                ALU.subtract).then_inc(xlo_d, 1)

                def group(g, more):
                    add_q(g, 16, 0, range(0, 2), 0)
                    dve.wait_ge(h_mm, g + 1)
                    nc.vector.tensor_tensor(h_own[:], ps[:, HBANK, 0:GT].rearrange("p (b s) -> p b s", b=GB),
                                            own[:].to_broadcast([P, GB, SEQ]), ALU.mult).then_inc(h_own_d, 1)
                    add_q(g, 16, 0, range(2, 3), 0)
                    dve.wait_ge(h_hi_d, g + 1)
                    nc.vector.tensor_tensor(h_lo[:], h_own[:].rearrange("p b s -> p (b s)"), h_hi[:].bitcast(F32),
                                            ALU.subtract).then_inc(h_lo_d, 1)
                    add_q(g, 16, 0, range(3, 16), 0)
                    if more:
                        split_x(g + 1)

                split_x(0)
                with dve.Fori(0, NG - 1) as g:
                    group(g, True)
                group(NG - 1, False)

        with ExitStack() as l1:
            aw_hi = sb("aw_hi", [P, KT, AW], F32R, l1)
            aw_lo = sb("aw_lo", [P, KT, AW], F32R, l1)
            b1_hi = sb("b1_hi", [P, D], F32R, l1)
            b1_lo = sb("b1_lo", [P, D], F32R, l1)
            with ExitStack() as ph:
                st = sb("st_w1", [P, 2, D], F32, ph)
                st_a = sb("st_a", [P, D], F32, ph)
                st_r = sb("st_r", [P, D], F32, ph)
                st_b = sb("st_b", [P, NE, KT, R], F32, ph)
                st_b2 = sb("st_b2", [P, KT, NE, R], F32, ph)
                prep1 = Prep("w1", W1, st, KT, False, prep_lo[1])
                a_ld, r_ld, b_ld = sem("a_ld"), sem("r_ld"), sem("b_ld")
                r_zero, b_perm = sem("r_zero"), sem("b_perm")
                a_tp, r_tp, b_tp = sem("a_tp"), sem("r_tp"), sem("b_tp")
                a_hi_d, a_lo_d = sem("a_hi_d"), sem("a_lo_d")
                s0_add = sem("s0_add")
                block = ph.enter_context(nc.Block())

                @block.sync
                def _(sp):
                    sp.dma_start(w3_upper.rearrange("(b p) n -> p b n", p=P), w3_sum[:]).then_inc(dma_w3, 16)
                    prep1.sync(sp)
                    sp.wait_ge(dma_w3, 32)
                    sp.dma_start(w3_sum[:], W3[HALF:D, :].rearrange("(b p) n -> p b n", p=P)).then_inc(dma_w3, 16)

                @block.gpsimd
                def _(pool):
                    nc.gpsimd.memset(st_r[:], 0.0).then_inc(r_zero, 1)
                    prep1.pool(pool)
                    pool.wait_ge(b_ld, 16)
                    nc.gpsimd.tensor_copy(st_b2[:], st_b[:].rearrange("p e j r -> p j e r")).then_inc(b_perm, 1)

                @block.scalar
                def _(act_e):
                    act_e.dma_start(st_a[:], A1.rearrange("e r n -> (e r) n")).then_inc(a_ld, 16)
                    act_e.dma_start(st_b[:].rearrange("p e j r -> p e (j r)"),
                                    B1.rearrange("e (p j) r -> p e (j r)", j=KT)).then_inc(b_ld, 16)
                    act_e.wait_ge(r_zero, 1)
                    act_e.dma_start(st_r[0:NE, :], Wr).then_inc(r_ld, 16)
                    prep1.scalar(act_e)
                    act_e.wait_ge(a_tp, 1)
                    nc.scalar.activation(aw_hi[:, :, 0:ER], tiles(4), ACT.Copy).then_inc(a_hi_d, 1)
                    act_e.wait_ge(r_tp, 1)
                    nc.scalar.activation(aw_hi[:, :, ER:AW], tiles(6)[:, :, 0:NE], ACT.Copy).then_inc(a_hi_d, 1)
                    act_e.wait_ge(b_tp, 1)
                    nc.scalar.activation(b1_hi[:].rearrange("q (p j) -> q j p", j=KT), tiles(4), ACT.Copy,
                                         scale=SCALING).then_inc(a_hi_d, 1)

                @block.tensor
                def _(pe):
                    prep1.tensor(pe)
                    for stage, ld, bank, done in ((st_a, a_ld, 4, a_tp), (st_r, r_ld, 6, r_tp)):
                        pe.wait_ge(ld, 16)
                        for k in range(KT):
                            last = nc.tensor.transpose(banks(bank)[:, k * P:(k + 1) * P],
                                                       stage[:, k * P:(k + 1) * P], ident[:])
                        last.then_inc(done, 1)
                    pe.wait_ge(b_perm, 1)
                    pe.wait_ge(a_lo_d, 1)
                    for j in range(KT):
                        last = nc.tensor.transpose(banks(4)[:, j * P:(j + 1) * P],
                                                   st_b2[:, j, :, :].rearrange("p e r -> p (e r)"), ident[:])
                    last.then_inc(b_tp, 1)

                @block.vector
                def _(dve):
                    prep1.vector(dve)
                    dve.wait_ge(a_hi_d, 1)
                    nc.vector.tensor_tensor(aw_lo[:, :, 0:ER], tiles(4), aw_hi[:, :, 0:ER].bitcast(F32),
                                            ALU.subtract).then_inc(a_lo_d, 1)
                    dve.wait_ge(a_hi_d, 2)
                    nc.vector.tensor_tensor(aw_lo[:, :, ER:AW], tiles(6)[:, :, 0:NE],
                                            aw_hi[:, :, ER:AW].bitcast(F32), ALU.subtract).then_inc(a_lo_d, 1)
                    dve.wait_ge(a_hi_d, 3)
                    perm = "q (p j) -> q j p"
                    nc.vector.scalar_tensor_tensor(
                        out=b1_lo[:].rearrange(perm, j=KT), in0=tiles(4), scalar=SCALING,
                        in1=b1_hi[:].bitcast(F32).rearrange(perm, j=KT),
                        op0=ALU.mult, op1=ALU.subtract).then_inc(a_lo_d, 1)
                    dve.wait_ge(dma_w3, 48)
                    nc.vector.tensor_scalar(w3_sum[:], w3_sum[:], s0[:, 0:1], None, ALU.add).then_inc(s0_add, 1)
                    dve.wait_ge(s0_add, 1)

            x1_hi = sb("x1_hi", [P, 2, KT, P], F32R, l1)
            x1_lo = sb("x1_lo", [P, KT, P], F32R, l1)
            x2_hi = sb("x2_hi", [P, D], F32R, l1)
            x2_lo = sb("x2_lo", [P, D], F32R, l1)
            w2_raw = sb("w2_raw", [P, 2, P], F32, l1)
            w2_id = sb("w2_id", [P, P], F32, l1)
            w2_hi = sb("w2_hi", [P, P], F32R, l1)
            w2_lo = sb("w2_lo", [P, P], F32R, l1)
            bias_bc = sb("bias_bc", [P, 2, 1, P], F32, l1)
            hg = sb("hg", [P, ER], F32, l1)
            hg_hi = sb("hg_hi", [P, P], F32R, l1)
            hg_lo = sb("hg_lo", [P, P], F32R, l1)
            logit = sb("logit", [P, NE], F32, l1)
            top = sb("top", [P, NE], F32, l1)
            top_i = sb("top_i", [P, NE], U32, l1)
            top_f = sb("top_f", [P, 2], F32, l1)
            gap = sb("gap", [P, 1], F32, l1)
            e_gap = sb("e_gap", [P, 1], F32, l1)
            e_sum = sb("e_sum", [P, 1], F32, l1)
            g_w = sb("g_w", [P, 2], F32, l1)
            g_one = sb("g_one", [P, 2, NE], F32, l1)
            gate = sb("gate", [P, NE, 1], F32, l1)
            H1, GT1, OUT2 = 4, 5, 6
            x1_hi_d, x1_lo_d = sem("x1_hi_d"), sem("x1_lo_d")
            h1_mm, hgt, y1_mm, l2_mm = (sem(n) for n in ("h1_mm", "hgt", "y1_mm", "l2_mm"))
            gs = sem("gs")
            GS = 11
            gap_exp, hg_hi_d, hg_lo_d = sem("gap_exp"), sem("hg_hi_d"), sem("hg_lo_d")
            x2_hi_d = sem("x2_hi_d")
            w2_zero, w2_ld = sem("w2_zero"), [sem(f"w2_ld{d}") for d in range(2)]
            w2_id_d, w2_hi_d, w2_lo_d = sem("w2_id_d"), sem("w2_hi_d"), sem("w2_lo_d")
            block = l1.enter_context(nc.Block())

            @block.sync
            def _(sp):
                per, n0 = 2 * L1_QT, L0_Q
                with sp.Fori(0, TT // 2) as it:
                    stream_q(sp, it, per, n0, range(per), 1)

            @block.gpsimd
            def _(pool):
                def load(it, d):
                    for c in range(2):
                        s = pool.value_load(subj_row[0:1, ds(it * 4 + (2 * d + c), 1)], min_val=0,
                                            max_val=w2.shape[0] - 1)
                        part = slice(c * SEQ, (c + 1) * SEQ)
                        pool.dma_start(w2_raw[part, d, part], w2[ds(s, 1), :, :].rearrange("a c n -> (a c) n"))\
                            .then_inc(w2_ld[d], 16)
                        pool.dma_start(bias_bc[:, d, 0, part],
                                       bias2[ds(s, 1), :, :].rearrange("a b n -> (a b) n").to_broadcast([P, SEQ]))\
                            .then_inc(w2_ld[d], 16)

                def tile(it, d, first=False):
                    pool.wait_ge(w2_ld[d], it * 64 + 64)
                    if not first:
                        pool.wait_ge(w2_lo_d, it * 2 + d)
                    pool.wait_ge(w2_hi_d, it * 2 + (d + 1))
                    nc.gpsimd.tensor_tensor(w2_id[:], w2_raw[:, d, :], ident[:], ALU.add).then_inc(w2_id_d, 1)
                    pool.wait_ge(w2_hi_d, it * 2 + (d + 2))
                    nc.gpsimd.tensor_tensor(w2_lo[:], w2_id[:], w2_hi[:].bitcast(F32), ALU.subtract)\
                        .then_inc(w2_lo_d, 1)

                def reload(it, d):
                    pool.wait_ge(x3_out, it * 2 + d)
                    load(it, d)

                nc.gpsimd.memset(w2_raw[:], 0.0).then_inc(w2_zero, 1)
                pool.sem_inc(w2_hi_d, 1)
                pool.wait_ge(w2_zero, 1)
                load(0, 0)
                load(0, 1)
                tile(0, 0, first=True)
                tile(0, 1)
                with pool.Fori(1, TT // 2) as it:
                    for d in range(2):
                        reload(it, d)
                        tile(it, d)

            @block.scalar
            def _(act_e):
                def split_x1(it, d):
                    if not (isinstance(it, int) and it == 0 and d == 0):
                        act_e.wait_ge(base_mm, it * 2 + d)
                    nc.scalar.activation(x1_hi[:, d, :, :], act[:, :, ds(it * 2 * P + d * P, P)], ACT.Copy)\
                      .then_inc(x1_hi_d, 1)

                def tile(it, d, nxt):
                    n1 = d + 1
                    if nxt:
                        split_x1(*nxt)
                    act_e.wait_ge(gs, it * (2 * GS) + (d * GS + 5))
                    nc.scalar.activation(e_gap[:], gap[:], ACT.Exp).then_inc(gap_exp, 1)
                    act_e.wait_ge(hgt, it * 2 + n1)
                    nc.scalar.activation(hg_hi[:], ps[:, GT1, 0:P], ACT.Copy).then_inc(hg_hi_d, 1)
                    act_e.wait_ge(y1_mm, it * 2 + n1)
                    nc.scalar.activation(x2_hi[:], banks(2 * d), ACT.Copy).then_inc(x2_hi_d, 1)
                    act_e.wait_ge(w2_id_d, it * 2 + n1)
                    nc.scalar.activation(w2_hi[:], w2_id[:], ACT.Copy).then_inc(w2_hi_d, 1)

                split_x1(0, 0)
                with act_e.Fori(0, TT // 2 - 1) as it:
                    tile(it, 0, (it, 1))
                    tile(it, 1, (it + 1, 0))
                tile(TT // 2 - 1, 0, (TT // 2 - 1, 1))
                tile(TT // 2 - 1, 1, None)

            @block.tensor
            def _(pe):
                def l2(it, d):
                    n1 = d + 1
                    pe.wait_ge(x2_lo_d, it * 2 + (n1 + 2))
                    pe.wait_ge(w2_lo_d, it * 2 + n1)
                    pe.wait_ge(x3_out, it * 2 + n1)
                    for k in range(KT):
                        cols = slice(k * P, (k + 1) * P)
                        for n, (a, b) in enumerate(((x2_hi, w2_hi), (x2_lo, w2_hi), (x2_hi, w2_lo))):
                            last = nc.tensor.matmul(banks(OUT2)[:, cols], a[:, cols], b[:],
                                                    start=(n == 0), stop=(n == 2))
                    last.then_inc(l2_mm, 1)

                def tile(it, d, prev):
                    n1 = d + 1
                    pe.wait_ge(x1_lo_d, it * 2 + n1)
                    xh, xl = x1_hi[:, d, :, :], x1_lo
                    for k in range(KT):
                        for n, (a, b) in enumerate(((xh, aw_hi), (xl, aw_hi), (xh, aw_lo))):
                            last = nc.tensor.matmul(ps[:, H1, 0:AW], a[:, k, :], b[:, k, :],
                                                    start=(k == 0 and n == 0), stop=(k == KT - 1 and n == 2))
                    last.then_inc(h1_mm, 1)
                    pe.wait_ge(x2_lo_d, it * 2 + n1)
                    for half in range(2):
                        cols = slice(half * NB, (half + 1) * NB)
                        for k in range(KT):
                            for n, (a, b) in enumerate(((xh, w_hi), (xl, w_hi), (xh, w_lo))):
                                last = nc.tensor.matmul(ps[:, 2 * d + half, :], a[:, k, :], b[:, k, cols],
                                                        start=(k == 0 and n == 0), stop=False)
                        if half == 0:
                            pe.wait_ge(gs, it * (2 * GS) + (d + 1) * GS)
                            nc.tensor.transpose(ps[:, GT1, 0:P], hg[:], ident[:]).then_inc(hgt, 1)
                    last.then_inc(base_mm, 1)
                    if prev:
                        l2(*prev)
                    pe.wait_ge(hg_lo_d, it * 2 + n1)
                    for half in range(2):
                        cols = slice(half * NB, (half + 1) * NB)
                        for n, (a, b) in enumerate(((hg_hi, b1_hi), (hg_lo, b1_hi), (hg_hi, b1_lo))):
                            last = nc.tensor.matmul(ps[:, 2 * d + half, :], a[:], b[:, cols],
                                                    start=False, stop=(n == 2))
                    last.then_inc(y1_mm, 1)

                tile(0, 0, None)
                tile(0, 1, (0, 0))
                with pe.Fori(1, TT // 2) as it:
                    tile(it, 0, (it - 1, 1))
                    tile(it, 1, (it, 0))
                l2(TT // 2 - 1, 1)

            @block.vector
            def _(dve):
                def split_x1(it, d, first=False):
                    dve.wait_ge(x1_hi_d, it * 2 + (d + 1))
                    if not first:
                        dve.wait_ge(base_mm, it * 2 + (d + 1))
                    nc.vector.tensor_tensor(x1_lo[:], act[:, :, ds(it * 2 * P + d * P, P)],
                                            x1_hi[:, d, :, :].bitcast(F32), ALU.subtract).then_inc(x1_lo_d, 1)

                def out_x3(it, d):
                    dve.wait_ge(l2_mm, it * 2 + (d + 1))
                    nc.vector.tensor_tensor(act[:, :, ds(it * 2 * P + d * P, P)], tiles(OUT2),
                                            bias_bc[:, d, :, :].to_broadcast([P, KT, P]), ALU.add).then_inc(x3_out, 1)

                def gating(it, d, add):
                    base = it * (2 * GS) + d * GS
                    step = lambda n: dve.wait_ge(gs, base + n)
                    dve.wait_ge(h1_mm, it * 2 + (d + 1))
                    nc.vector.tensor_tensor(logit[:], ps[:, H1, ER:AW],
                                            lang_bias[:, ds(it * 2 + d, 1), :].rearrange("p a e -> p (a e)"),
                                            ALU.add).then_inc(gs, 1)
                    step(1)
                    add(0)
                    nc.vector.max(top[:], logit[:]).then_inc(gs, 1)
                    step(2)
                    add(1)
                    nc.vector.max_index(top_i[:], top[:], logit[:]).then_inc(gs, 1)
                    step(3)
                    nc.vector.tensor_copy(top_f[:], top_i[:, 0:2]).then_inc(gs, 1)
                    nc.vector.tensor_tensor(gap[:], top[:, 1:2], top[:, 0:1], ALU.subtract).then_inc(gs, 1)
                    dve.wait_ge(gap_exp, it * 2 + (d + 1))
                    nc.vector.tensor_scalar(e_sum[:], e_gap[:], 1.0, None, ALU.add).then_inc(gs, 1)
                    step(6)
                    nc.vector.reciprocal(g_w[:, 0:1], e_sum[:]).then_inc(gs, 1)
                    step(7)
                    nc.vector.tensor_tensor(g_w[:, 1:2], g_w[:, 0:1], e_gap[:], ALU.mult).then_inc(gs, 1)
                    step(8)
                    for i in range(2):
                        last = nc.vector.tensor_scalar(g_one[:, i, :], iota8[:], top_f[:, i:i + 1], g_w[:, i:i + 1],
                                                       ALU.is_equal, ALU.mult)
                    last.then_inc(gs, 1)
                    step(9)
                    nc.vector.tensor_tensor(gate[:, :, 0], g_one[:, 0, :], g_one[:, 1, :], ALU.add).then_inc(gs, 1)
                    step(10)
                    nc.vector.tensor_tensor(hg[:].rearrange("p (e r) -> p e r", e=NE),
                                            ps[:, H1, 0:ER].rearrange("p (e r) -> p e r", e=NE),
                                            gate[:].to_broadcast([P, NE, R]), ALU.mult).then_inc(gs, 1)

                def tile(it, d, prev, nxt):
                    q = (it, 2 * L1_QT, L0_Q)
                    gating(it, d, lambda j: add_q(*q, range(d * L1_QT + j, d * L1_QT + j + 1), 1))
                    add_q(*q, range(d * L1_QT + 2, d * L1_QT + 4), 1)
                    dve.wait_ge(hg_hi_d, it * 2 + (d + 1))
                    nc.vector.tensor_tensor(hg_lo[:], ps[:, GT1, 0:P], hg_hi[:].bitcast(F32), ALU.subtract)\
                      .then_inc(hg_lo_d, 1)
                    add_q(*q, range(d * L1_QT + 4, (d + 1) * L1_QT), 1)
                    if nxt:
                        split_x1(*nxt)
                    if prev:
                        out_x3(*prev)
                    dve.wait_ge(x2_hi_d, it * 2 + (d + 1))
                    nc.vector.tensor_tensor(x2_lo[:], banks(2 * d), x2_hi[:].bitcast(F32), ALU.subtract)\
                      .then_inc(x2_lo_d, 1)

                last = TT // 2 - 1
                split_x1(0, 0, first=True)
                tile(0, 0, None, (0, 1))
                tile(0, 1, (0, 0), (1, 0))
                with dve.Fori(1, last) as it:
                    tile(it, 0, (it - 1, 1), (it, 1))
                    tile(it, 1, (it, 0), (it + 1, 0))
                tile(last, 0, (last - 1, 1), (last, 1))
                tile(last, 1, (last, 0), None)
                out_x3(last, 1)

        with ExitStack() as l3:
            b3_bc = sb("b3_bc", [P, D], F32, l3)
            with ExitStack() as ph:
                st = sb("st_w3", [P, 2, D], F32, ph)
                bq_i = sb("bq_i", [NQ, D], I32, ph)
                bq_f = sb("bq_f", [NQ, D], F32, ph)
                sc_col = sb("sc_col", [NQ, 2], F32, ph)
                cb = sb("cb", [NQ, 1], F32, ph)
                cb_bc = sb("cb_bc", [NQ, P], F32, ph)
                ones = sb("ones", [NQ, P], F32, ph)
                prep3 = Prep("w3", w3_upper, st, HB, False, prep_lo[2])
                b3_ld, b3_s, b3_mm, bq_cv, b3_out = (sem(n) for n in ("b3_ld", "b3_s", "b3_mm", "bq_cv", "b3_out"))
                block = ph.enter_context(nc.Block())

                @block.sync
                def _(sp):
                    prep3.sync(sp)

                @block.gpsimd
                def _(pool):
                    prep3.pool(pool)

                @block.scalar
                def _(act_e):
                    act_e.dma_start(bq_i[:], bq).then_inc(b3_ld, 16)
                    act_e.dma_start(sc_col[:, 0:1], scale.rearrange("(n a) -> n a", a=1)).then_inc(b3_ld, 16)
                    act_e.dma_start(sc_col[:, 1:2], bscale.rearrange("(n a) -> n a", a=1)).then_inc(b3_ld, 16)
                    act_e.dma_start(b3_bc[:], row(b3).to_broadcast([P, D])).then_inc(b3_ld, 16)
                    act_e.wait_ge(b3_ld, 64)
                    nc.scalar.activation(bq_f[:], bq_i[:], ACT.Copy).then_inc(bq_cv, 1)
                    prep3.scalar(act_e)

                @block.tensor
                def _(pe):
                    pe.wait_ge(b3_s, 3)
                    pe.wait_ge(bq_cv, 1)
                    for half in range(2):
                        cols = slice(half * NB, (half + 1) * NB)
                        last = nc.tensor.matmul(ps[:, 4 + half, :], cb_bc[:], bq_f[:, cols], start=True, stop=True)
                    last.then_inc(b3_mm, 1)
                    prep3.tensor(pe)

                @block.vector
                def _(dve):
                    nc.vector.memset(ones[:], 1.0).then_inc(b3_s, 1)
                    dve.wait_ge(b3_ld, 64)
                    nc.vector.tensor_tensor(cb[:], sc_col[:, 0:1], sc_col[:, 1:2], ALU.mult).then_inc(b3_s, 1)
                    dve.wait_ge(b3_s, 2)
                    nc.vector.tensor_scalar(cb_bc[:], ones[:], cb[:, 0:1], None, ALU.mult).then_inc(b3_s, 1)
                    dve.wait_ge(b3_mm, 1)
                    nc.vector.scalar_tensor_tensor(out=b3_bc[:], in0=banks(4), scalar=s0[:, 0:1], in1=b3_bc[:],
                                                   op0=ALU.add, op1=ALU.add).then_inc(b3_out, 1)
                    prep3.vector(dve)

            x3_hi = sb("x3_hi", [P, 2, KT, P], F32R, l3)
            x3_lo = sb("x3_lo", [P, 2, KT, P], F32R, l3)
            y_sb = sb("y_sb", [P, 2, NB], F32, l3)
            for half in range(2):
                name = ("up", "low")[half]
                if half:
                    low_id, low_tp, low_hi, low_lo = (sem(n) for n in ("low_id", "low_tp", "low_hi", "low_lo"))
                    with nc.Block() as block:

                        @block.gpsimd
                        def _(pool):
                            for b in range(HB):
                                diag = w3_sum[:, b, (HB + b) * P:(HB + b + 1) * P]
                                nc.gpsimd.tensor_tensor(diag, diag, ident[:], ALU.add).then_inc(low_id, 1)

                        @block.tensor
                        def _(pe):
                            for b in range(HB):
                                pe.wait_ge(low_id, b + 1)
                                for k in range(KT):
                                    last = nc.tensor.transpose(banks(2 * b)[:, k * P:(k + 1) * P],
                                                               w3_sum[:, b, k * P:(k + 1) * P], ident[:])
                                last.then_inc(low_tp, 1)

                        @block.scalar
                        def _(act_e):
                            for b in range(HB):
                                act_e.wait_ge(low_tp, b + 1)
                                nc.scalar.activation(w_hi[:, :, (HB + b) * P:(HB + b + 1) * P], tiles(2 * b), ACT.Copy)\
                                  .then_inc(low_hi, 1)

                        @block.vector
                        def _(dve):
                            for b in range(HB):
                                dve.wait_ge(low_hi, b + 1)
                                o = slice((HB + b) * P, (HB + b + 1) * P)
                                nc.vector.tensor_tensor(w_lo[:, :, o], tiles(2 * b), w_hi[:, :, o].bitcast(F32),
                                                        ALU.subtract).then_inc(low_lo, 1)
                            dve.wait_ge(low_lo, HB)

                x3_hi_d, x3_lo_d, y3_mm = sem(f"x3_hi_d_{name}"), sem(f"x3_lo_d_{name}"), sem(f"y3_mm_{name}")
                y3_out, y3_st = y3_out_sems[half], [sem(f"y3_st{d}_{name}") for d in range(2)]
                per, n0 = 2 * L3_QT, L0_Q + TT * L1_QT
                LAST = TT // 2 - 1
                with nc.Block() as block:

                    @block.sync
                    def _(sp):
                        if half == 0:
                            with sp.Fori(0, LAST) as it:
                                stream_q(sp, it, per, n0, range(per), 1)

                    @block.gpsimd
                    def _(pool):
                        with pool.Fori(0, TT // 2) as it:
                            for d in range(2):
                                pool.wait_ge(y3_out, it * 2 + (d + 3))
                                pool.dma_start(y_rows[ds(it * 2 * P + d * P, P), half * NB:(half + 1) * NB],
                                               y_sb[:, d, :]).then_inc(y3_st[d], 16)
                        for d in range(2):
                            pool.wait_ge(y3_st[d], 16 * (TT // 2))

                    @block.scalar
                    def _(act_e):
                        def split(it, d):
                            if not (isinstance(it, int) and it == 0):
                                act_e.wait_ge(y3_mm, it * 2 + (d - 1))
                            nc.scalar.activation(x3_hi[:, d, :, :], act[:, :, ds(it * 2 * P + d * P, P)], ACT.Copy)\
                              .then_inc(x3_hi_d, 1)
                        for d in range(2):
                            split(0, d)
                        with act_e.Fori(1, TT // 2) as it:
                            for d in range(2):
                                split(it, d)

                    @block.tensor
                    def _(pe):
                        with pe.Fori(0, TT // 2) as it:
                            for d in range(2):
                                pe.wait_ge(x3_lo_d, it * 2 + (d + 1))
                                pe.wait_ge(y3_out, it * 2 + (d + 1))
                                xh, xl = x3_hi[:, d, :, :], x3_lo[:, d, :, :]
                                cols = slice(half * NB, (half + 1) * NB)
                                for k in range(KT):
                                    for n, (a, b) in enumerate(((xh, w_hi), (xl, w_hi), (xh, w_lo))):
                                        last = nc.tensor.matmul(ps[:, d, :], a[:, k, :], b[:, k, cols],
                                                                start=(k == 0 and n == 0), stop=(k == KT - 1 and n == 2))
                                last.then_inc(y3_mm, 1)

                    @block.vector
                    def _(dve):
                        def split(it, d):
                            dve.wait_ge(x3_hi_d, it * 2 + (d + 1))
                            nc.vector.tensor_tensor(x3_lo[:, d, :, :], act[:, :, ds(it * 2 * P + d * P, P)],
                                                    x3_hi[:, d, :, :].bitcast(F32), ALU.subtract).then_inc(x3_lo_d, 1)

                        def tile(it, d, first, nxt):
                            if nxt:
                                split(*nxt)
                            if half == 0:
                                add_q(it, per, n0, range(d * L3_QT, (d + 1) * L3_QT), 1)
                            dve.wait_ge(y3_mm, it * 2 + (d + 1))
                            if not first:
                                dve.wait_ge(y3_st[d], it * 16)
                            nc.vector.tensor_tensor(y_sb[:, d, :], ps[:, d, :], b3_bc[:, half * NB:(half + 1) * NB],
                                                    ALU.add).then_inc(y3_out, 1)

                        split(0, 0)
                        tile(0, 0, True, (0, 1))
                        tile(0, 1, True, (1, 0))
                        with dve.Fori(1, LAST) as it:
                            tile(it, 0, False, (it, 1))
                            tile(it, 1, False, (it + 1, 0))
                        tile(LAST, 0, False, (LAST, 1))
                        tile(LAST, 1, False, None)


_INS = ["x", "condB_scale", "condB_wscale", "condB_bscale", "_lenS", "itok_B_0_23", "itok_B_0_7",
        "itok_B_0_31", "itok_Bx4096x4096_0_255", "itok_Bx4096_0_255", "L0_cond_W", "L0_cond_b",
        "L0_cond_lora_As", "L0_cond_lora_Bs", "L1_cond_W", "L1_cond_Wr", "L1_cond_A", "L1_cond_B",
        "L2_cond_weights", "L2_cond_biases", "L3_cond_weight", "L3_cond_bias"]


def kernel(**inputs):
    import numpy as np
    import concourse.bacc as bacc
    from concourse.bass_utils import run_bass_kernel_spmd

    nc = bacc.Bacc("TRN2", target_bir_lowering=False, num_devices=1)
    arrays, args = {}, []
    for name in _INS:
        a = np.ascontiguousarray(inputs[name])
        arrays[f"in_{name}"] = a
        args.append(nc.dram_tensor(f"in_{name}", a.shape, mybir.dt.from_np(a.dtype), kind="ExternalInput").ap())
    args.append(nc.dram_tensor("out", (BATCH, SEQ, D), F32, kind="ExternalOutput").ap())
    program(nc, *args)
    return run_bass_kernel_spmd(nc, [arrays], core_ids=[0]).results[0]["out"]
```

```python
from contextlib import ExitStack

import concourse.bass as bass
from concourse import mybir

F32 = mybir.dt.float32
F32R = mybir.dt.float32r
I32 = mybir.dt.int32
U32 = mybir.dt.uint32
ALU = mybir.AluOpType
ACT = mybir.ActivationFunctionType
AX_X = mybir.AxisListType.X
ds = bass.ds

P = 128
BATCH, SEQ, D = 32, 64, 1024
T = BATCH * SEQ
KT = D // P
TT = T // P
GT = 256
NG = T // GT
GB = GT // SEQ
R = 16
NE = 8
ER = NE * R
AW = ER + NE
NB = 512
NQ = 32
HB = 4
HALF = HB * P
RING = 4
ST = 4
UP_Q = NQ * HB
L0_QG = 12
L0_Q = NG * L0_QG
L1_QT = 8
L3_QT = 2
L1_UP = (UP_Q - L0_Q) // (2 * L1_QT)
LANG_BIAS = 5.0
SCALING = 2.0
assert L0_Q + L1_UP * 2 * L1_QT == UP_Q and L0_Q + TT * (L1_QT + L3_QT) == 2 * UP_Q


def program(nc, x, scale, wscale, bscale, len_s, slot_id, lang_id, subj_id, wq, bq,
            W0, b0, lora_A, lora_B, W1, Wr, A1, B1, w2, bias2, W3, b3, y):
    w3_upper = nc.dram_tensor("w3_upper", (HALF, D), F32, kind="Internal").ap()
    x_rows = x.rearrange("b s d -> (b s) d")
    y_rows = y.rearrange("b s d -> (b s) d")
    lora_A_v = lora_A.rearrange("s (p k) r -> s p (k r)", k=KT)
    row = lambda v: v.rearrange("(a n) -> a n", a=1)

    with ExitStack() as ctx:
        def sb(name, shape, dt=F32, where=ctx):
            return where.enter_context(nc.sbuf_tensor(name, shape, dt))

        def sem(name):
            return ctx.enter_context(nc.semaphore(name))

        ident = sb("ident", [P, P])
        act = sb("act", [P, KT, T])
        w3_sum = sb("w3_sum", [P, HB, D])
        ring = sb("ring", [P, RING, D], I32)
        coef = sb("coef", [P, NQ])
        s0 = sb("s0", [P, 1])
        b0_col = sb("b0_col", [P, KT])
        lang_bias = sb("lang_bias", [P, TT, NE])
        iota8 = sb("iota8", [P, NE])
        subj_row = sb("subj_row", [1, BATCH], I32)
        slot_row = sb("slot_row", [1, BATCH], I32)
        own = sb("own", [P, GB, 1])
        ps = ctx.enter_context(nc.psum_tensor("ps", [P, 8, NB], F32))

        def banks(b):
            return ps[:, b:b + 2, :].rearrange("p b n -> p (b n)")

        def tiles(b):
            return ps[:, b:b + 2, :].rearrange("p b (k n) -> p (b k) n", n=P)

        ring_ld = [sem(f"ring_ld{s}") for s in range(RING)]
        sum_done = sem("sum_done")
        y_out = sem("y_out")
        x2_d = sem("x2_d")
        x3_out = sem("x3_out")
        y3_out = sem("y3_out")
        prep_lo = [sem(f"prep_lo{n}") for n in range(3)]
        base_mm = sem("base_mm")
        begin_with = {sum_done: RING, y_out: 2, x2_d: 2, y3_out: 2, x3_out: 1, base_mm: 1}
        begin_with.update({s: ST for s in prep_lo})
        w3_ld = sem("w3_ld")
        up_st = [sem(f"up_st{b}") for b in range(HB)]

        def load_q(eng, block, expert, half):
            r0 = half * HALF + block * P
            eng.dma_start(ring[:, block, :], wq[ds(expert, 1), r0:r0 + P, :]
                          .rearrange("a p n -> p (a n)")).then_inc(ring_ld[block], 16)

        def stream_q(eng, it, per, n0, js, half):
            for j in js:
                eng.wait_ge(sum_done, it * per + (n0 + j + RING + 1))
                load_q(eng, j % RING, it * (per // RING) + (n0 - half * UP_Q + j + RING) // RING, half)

        def add_q(it, per, n0, js, half):
            for j in js:
                s = j % RING
                nc.vector.wait_ge(ring_ld[s], it * (4 * per) + 16 * ((n0 + j) // RING + 1))
                nc.vector.wait_ge(sum_done, it * per + (n0 + j + 1))
                expert = it * (per // RING) + (n0 - half * UP_Q + j) // RING
                nc.vector.scalar_tensor_tensor(
                    out=w3_sum[:, s, :], in0=ring[:, s, :], scalar=coef[:, ds(expert, 1)],
                    in1=w3_sum[:, s, :], op0=ALU.mult, op1=ALU.add).then_inc(sum_done, 1)

        class Prep:

            def __init__(self, name, w, st, blocks, w_hi, w_lo, lo, strided=False, first=0, col0=0):
                self.w, self.st, self.n, self.strided = w, st, blocks, strided
                self.w_hi, self.w_lo, self.first, self.col0 = w_hi, w_lo, first, col0
                self.st_ld = [sem(f"{name}_ld{d}") for d in range(ST)]
                self.st_id = sem(f"{name}_id")
                self.tp = sem(f"{name}_tp")
                self.hi = sem(f"{name}_hi")
                self.lo = lo

            def load(self, eng, n):
                if n >= ST:
                    eng.wait_ge(self.tp, self.first + n - ST + 1)
                eng.dma_start(self.st[:, n % ST, :], self.w[n * P:(n + 1) * P, :]).then_inc(self.st_ld[n % ST], 16)

            def to_banks(self, pair, src):
                for k in range(KT):
                    last = nc.tensor.transpose(banks(2 * pair)[:, k * P:(k + 1) * P], src(k), ident[:])
                last.then_inc(self.tp, 1)

            def pool(self, eng):
                with eng.Fori(0, self.n // ST) as it:
                    for d in range(ST):
                        eng.wait_ge(self.st_ld[d], it * 16 + 16)
                        diag = self.st[:, d, ds(it * (ST * P) + d * P, P)]
                        nc.gpsimd.tensor_tensor(diag, diag, ident[:], ALU.add).then_inc(self.st_id, 1)

            def tensor(self, eng):
                with eng.Fori(0, self.n // ST) as it:
                    for d in range(ST):
                        eng.wait_ge(self.st_id, it * ST + (d + 1))
                        eng.wait_ge(self.lo, it * ST + (self.first + d + 1))
                        self.to_banks(d, lambda k: self.st[:, d, k::KT] if self.strided
                                      else self.st[:, d, k * P:(k + 1) * P])

            def scalar(self, eng):
                with eng.Fori(0, self.n // ST) as it:
                    for d in range(ST):
                        eng.wait_ge(self.tp, it * ST + (self.first + d + 1))
                        nc.scalar.activation(self.w_hi[:, :, ds(it * (ST * P) + (self.col0 + d * P), P)],
                                             tiles(2 * d), ACT.Copy).then_inc(self.hi, 1)

            def vector(self, eng):
                with eng.Fori(0, self.n // ST) as it:
                    for d in range(ST):
                        eng.wait_ge(self.hi, it * ST + (self.first + d + 1))
                        o = ds(it * (ST * P) + (self.col0 + d * P), P)
                        nc.vector.tensor_tensor(self.w_lo[:, :, o], tiles(2 * d), self.w_hi[:, :, o].bitcast(F32),
                                                ALU.subtract).then_inc(self.lo, 1)

        stage = ring[:].bitcast(F32)

        with ExitStack() as ph:
            w_hi = sb("w0_hi", [P, KT, D], F32R, ph)
            w_lo = sb("w0_lo", [P, KT, D], F32R, ph)
            x_in = sb("x_in", [P, 2, D], F32, ph)
            A_raw = sb("A_raw", [P, GB, KT * R], F32, ph)
            B_raw = sb("B_raw", [P, D], F32, ph)
            xT_hi = sb("xT_hi", [P, KT, GT], F32R, ph)
            xT_lo = sb("xT_lo", [P, KT, GT], F32R, ph)
            A_hi = sb("A_hi", [P, KT, P], F32R, ph)
            A_lo = sb("A_lo", [P, KT, P], F32R, ph)
            B_st = sb("B_st", [P, D], F32R, ph)
            h_own = sb("h_own", [P, GB, SEQ], F32, ph)
            h_hi = sb("h_hi", [P, GT], F32R, ph)
            h_lo = sb("h_lo", [P, GT], F32R, ph)
            scale_bc = sb("scale_bc", [P, NQ], F32, ph)
            wscale_bc = sb("wscale_bc", [P, NQ], F32, ph)
            len_bc = sb("len_bc", [P, NQ], I32, ph)
            len_f = sb("len_f", [P, NQ], F32, ph)
            lang_bc = sb("lang_bc", [P, BATCH], I32, ph)
            lang_tt = sb("lang_tt", [P, TT, 1], F32, ph)
            same = sb("same", [P, 2 * GB], F32, ph)
            PAIRS = KT // 2
            HBANK = 6
            Y = [(4, 5, 7)[o % 3] for o in range(KT)]
            x_ld = [sem(f"x_ld{d}") for d in range(2)]
            A_ld, B_ld = sem("A_ld"), sem("B_ld")
            consts_ld, rows_ld = sem("consts_ld"), sem("rows_ld")
            len_d = sem("len_d")
            cst = sem("cst")
            dve_s = sem("dve_s")
            A_hi_d, A_lo_d, B_hi_d, B_lo_d = sem("A_hi_d"), sem("A_lo_d"), sem("B_hi_d"), sem("B_lo_d")
            xtp = sem("xtp")
            xhi_d, xlo_d = sem("xhi_d"), sem("xlo_d")
            x_used = sem("x_used")
            h_mm, h_own_d, h_hi_d, h_lo_d = sem("h_mm"), sem("h_own_d"), sem("h_hi_d"), sem("h_lo_d")
            w3_s0 = sem("w3_s0")
            y_mm = sem("y_mm")
            prep0 = Prep("w0", W0, stage, KT, w_hi, w_lo, prep_lo[0], strided=True)
            prep1 = Prep("w1", W1, stage, KT, None, None, prep_lo[1], col0=AW)
            block = ph.enter_context(nc.Block())

            @block.sync
            def _(sp):
                def load_x(g):
                    for d in range(2):
                        sp.dma_start(x_in[:, d, :], x_rows[ds(g * GT + d * P, P), :]).then_inc(x_ld[d], 16)

                def load_adapters(g):
                    for b in range(GB):
                        s = sp.value_load(slot_row[0:1, ds(g * GB + b, 1)], min_val=0, max_val=lora_A.shape[0] - 1)
                        sp.dma_start(A_raw[:, b, :], lora_A_v[ds(s, 1), :, :].rearrange("a p n -> p (a n)"))\
                          .then_inc(A_ld, 16)
                        for copy in range(2):
                            r0 = copy * GB * R + b * R
                            sp.dma_start(B_raw[r0:r0 + R, :], lora_B[ds(s, 1), :, :].rearrange("a r n -> (a r) n"))\
                              .then_inc(B_ld, 16)

                for n in range(KT):
                    prep0.load(sp, n)
                load_x(0)
                sp.wait_ge(rows_ld, 48)
                load_adapters(0)
                for b in range(HB):
                    sp.wait_ge(prep0.tp, KT - ST + b + 1)
                    load_q(sp, b, 0, 0)
                sp.dma_start(w3_sum[:], W3[0:HALF, :].rearrange("(b p) n -> p b n", p=P)).then_inc(w3_ld, 16)
                with sp.Fori(0, NG - 1) as g:
                    stream_q(sp, g, L0_QG, 0, range(2), 0)
                    sp.wait_ge(xtp, g * PAIRS + PAIRS)
                    load_x(g + 1)
                    stream_q(sp, g, L0_QG, 0, range(2, 5), 0)
                    sp.wait_ge(A_lo_d, g + 1)
                    sp.wait_ge(B_lo_d, g + 1)
                    load_adapters(g + 1)
                    stream_q(sp, g, L0_QG, 0, range(5, L0_QG), 0)
                stream_q(sp, NG - 1, L0_QG, 0, range(L0_QG - RING), 0)
                for b in range(ST):
                    sp.wait_ge(sum_done, L0_Q + b + 1)
                    prep1.load(sp, b)

            @block.gpsimd
            def _(pool):
                nc.gpsimd.memset(ident[:], 0.0).then_inc(cst, 1)
                pool.wait_ge(cst, 1)
                nc.gpsimd.affine_select(out=ident[:], in_=ident[:], compare_op=ALU.not_equal, fill=1.0, base=0,
                                        pattern=[[-1, P]], channel_multiplier=1).then_inc(cst, 1)
                for s, count in begin_with.items():
                    pool.sem_inc(s, count)
                nc.gpsimd.memset(same[:], SCALING).then_inc(cst, 1)
                pool.wait_ge(cst, 3)
                nc.gpsimd.affine_select(out=same[:], in_=same[:], compare_op=ALU.is_ge, fill=0.0, base=0,
                                        pattern=[[-R, 2 * GB]], channel_multiplier=1).then_inc(cst, 1)
                pool.wait_ge(cst, 4)
                nc.gpsimd.affine_select(out=same[:], in_=same[:], compare_op=ALU.is_ge, fill=0.0, base=R - 1,
                                        pattern=[[R, 2 * GB]], channel_multiplier=-1).then_inc(cst, 1)
                pool.wait_ge(cst, 5)
                nc.gpsimd.tensor_tensor(own[:, :, 0], same[:, 0:GB], same[:, GB:2 * GB], ALU.add).then_inc(cst, 1)
                prep0.pool(pool)
                nc.gpsimd.iota(iota8[:], pattern=[[1, NE]], base=0, channel_multiplier=0,
                               allow_small_or_imprecise_dtypes=True).then_inc(cst, 1)
                pool.wait_ge(rows_ld, 48)

                def split_A(g):
                    pool.wait_ge(A_hi_d, g + 1)
                    raw = A_raw[:].rearrange("p b (k r) -> p k b r", k=KT)
                    for copy in range(2):
                        cols = slice(copy * GB * R, (copy + 1) * GB * R)
                        hi = A_hi[:, :, cols].bitcast(F32).rearrange("p k (b r) -> p k b r", b=GB)
                        lo = A_lo[:, :, cols].rearrange("p k (b r) -> p k b r", b=GB)
                        last = nc.gpsimd.tensor_tensor(lo, raw, hi, ALU.subtract)
                    last.then_inc(A_lo_d, 1)

                def split_B(g):
                    pool.wait_ge(A_lo_d, g + 1)
                    pool.wait_ge(B_hi_d, g + 1)
                    low = slice(GB * R, P)
                    nc.gpsimd.tensor_tensor(B_st[low, :], B_raw[low, :], B_st[low, :].bitcast(F32),
                                            ALU.subtract).then_inc(B_lo_d, 1)

                split_A(0)
                split_B(0)
                with pool.Fori(0, NG - 1) as g:
                    pool.wait_ge(B_lo_d, g + 1)
                    split_A(g + 1)
                    split_B(g + 1)

            @block.scalar
            def _(act_e):
                act_e.dma_start(slot_row[:], row(slot_id)).then_inc(rows_ld, 16)
                act_e.dma_start(subj_row[:], row(subj_id)).then_inc(rows_ld, 16)
                with nc.allow_non_contiguous_dma(reason="1024 values of the bias, once"):
                    act_e.dma_start(b0_col[:], b0.rearrange("(k p) -> p k", p=P)).then_inc(rows_ld, 16)
                for dst, src in ((scale_bc, scale), (wscale_bc, wscale), (len_bc, len_s), (lang_bc, lang_id)):
                    act_e.dma_start(dst[:], row(src).to_broadcast([P, NQ])).then_inc(consts_ld, 16)
                act_e.wait_ge(rows_ld, 48)
                act_e.wait_ge(consts_ld, 64)
                nc.scalar.activation(len_f[:], len_bc[:], ACT.Copy).then_inc(len_d, 1)
                prep0.scalar(act_e)

                def split_A(g):
                    act_e.wait_ge(A_ld, g * (16 * GB) + 16 * GB)
                    raw = A_raw[:].rearrange("p b (k r) -> p k b r", k=KT)
                    for copy in range(2):
                        cols = slice(copy * GB * R, (copy + 1) * GB * R)
                        last = nc.scalar.activation(A_hi[:, :, cols].rearrange("p k (b r) -> p k b r", b=GB),
                                                    raw, ACT.Copy)
                    last.then_inc(A_hi_d, 1)

                def split_B(g):
                    act_e.wait_ge(B_ld, g * (32 * GB) + 32 * GB)
                    nc.scalar.activation(B_st[:], B_raw[:], ACT.Copy).then_inc(B_hi_d, 1)

                def split_x(g):
                    for j in range(PAIRS):
                        act_e.wait_ge(xtp, g * PAIRS + (j + 1))
                        if not (isinstance(g, int) and g == 0):
                            act_e.wait_ge(x_used, (g - 1) * PAIRS + (j + 1))
                        nc.scalar.activation(xT_hi[:, 2 * j:2 * j + 2, :].rearrange("p k t -> p (k t)"),
                                             ps[:, j, :], ACT.Copy).then_inc(xhi_d, 1)

                def out(g, o):
                    act_e.wait_ge(y_mm, g * KT + (o + 1))
                    nc.scalar.activation(act[:, o, ds(g * GT, GT)], ps[:, Y[o], 0:GT], ACT.Identity,
                                         bias=b0_col[:, o:o + 1]).then_inc(y_out, 1)

                def group(g, more):
                    act_e.wait_ge(h_own_d, g + 1)
                    nc.scalar.activation(h_hi[:], h_own[:].rearrange("p b s -> p (b s)"), ACT.Copy)\
                      .then_inc(h_hi_d, 1)
                    for o in range(6):
                        out(g, o)
                    if more:
                        split_A(g + 1)
                    out(g, 6)
                    if more:
                        split_x(g + 1)
                    out(g, KT - 1)
                    if more:
                        split_B(g + 1)

                split_x(0)
                split_A(0)
                split_B(0)
                with act_e.Fori(0, NG - 1) as g:
                    group(g, True)
                group(NG - 1, False)

            @block.tensor
            def _(pe):
                pe.wait_ge(cst, 2)
                prep0.tensor(pe)

                def transpose_x(g):
                    for d in range(2):
                        pe.wait_ge(x_ld[d], g * 16 + 16)
                    for j in range(PAIRS):
                        for k in (2 * j, 2 * j + 1):
                            for d in range(2):
                                c = (k % 2) * GT + d * P
                                last = nc.tensor.transpose(ps[:, j, c:c + P], x_in[:, d, k::KT], ident[:])
                        last.then_inc(xtp, 1)

                def group(g, more):
                    pe.wait_ge(A_lo_d, g + 1)
                    for k in range(KT):
                        if k % 2 == 0:
                            pe.wait_ge(xlo_d, g * PAIRS + (k // 2 + 1))
                        for n, (a, b) in enumerate(((A_hi, xT_hi), (A_lo, xT_hi), (A_hi, xT_lo))):
                            last = nc.tensor.matmul(ps[:, HBANK, 0:GT], a[:, k, :], b[:, k, :],
                                                    start=(k == 0 and n == 0), stop=(k == KT - 1 and n == 2))
                    last.then_inc(h_mm, 1)

                    def base(o):
                        pe.wait_ge(y_out, g * KT + (o + 1 if o < 2 else o))
                        cols = slice(o * P, (o + 1) * P)
                        for k in range(KT):
                            for n, (a, b) in enumerate(((w_hi, xT_hi), (w_lo, xT_hi), (w_hi, xT_lo))):
                                last = nc.tensor.matmul(ps[:, Y[o], 0:GT], a[:, k, cols], b[:, k, :],
                                                        start=(k == 0 and n == 0), stop=False)
                            if o == KT - 1 and k % 2:
                                last.then_inc(x_used, 1)

                    def lora(o):
                        cols = slice(o * P, (o + 1) * P)
                        nc.tensor.matmul(ps[:, Y[o], 0:GT], B_st[:, cols], h_hi[:], start=False, stop=False)
                        nc.tensor.matmul(ps[:, Y[o], 0:GT], B_st[:, cols], h_lo[:], start=False, stop=True)\
                          .then_inc(y_mm, 1)

                    base(0)
                    base(1)
                    pe.wait_ge(h_lo_d, g + 1)
                    pe.wait_ge(B_lo_d, g + 1)
                    lora(0)
                    lora(1)
                    for o in range(2, KT):
                        base(o)
                        lora(o)
                        if o == 4 and more:
                            transpose_x(g + 1)

                pe.wait_ge(prep0.lo, ST + KT)
                transpose_x(0)
                with pe.Fori(0, NG - 1) as g:
                    group(g, True)
                group(NG - 1, False)

            @block.vector
            def _(dve):
                dve.wait_ge(consts_ld, 64)
                nc.vector.tensor_tensor(coef[:], scale_bc[:], wscale_bc[:], ALU.mult).then_inc(dve_s, 1)
                half = P // 2
                nc.vector.tensor_copy(lang_tt[0:half, :, 0], lang_bc[0:half, 0::2]).then_inc(dve_s, 1)
                nc.vector.tensor_copy(lang_tt[half:P, :, 0], lang_bc[half:P, 1::2]).then_inc(dve_s, 1)
                dve.wait_ge(len_d, 1)
                nc.vector.tensor_tensor(len_f[:], len_f[:], scale_bc[:], ALU.mult).then_inc(dve_s, 1)
                dve.wait_ge(dve_s, 4)
                nc.vector.reduce_sum(s0[:], len_f[:], AX_X).then_inc(dve_s, 1)
                prep0.vector(dve)

                def split_x(g):
                    for j in range(PAIRS):
                        dve.wait_ge(xhi_d, g * PAIRS + (j + 1))
                        pair = slice(2 * j, 2 * j + 2)
                        nc.vector.tensor_tensor(xT_lo[:, pair, :].rearrange("p k t -> p (k t)"), ps[:, j, :],
                                                xT_hi[:, pair, :].bitcast(F32).rearrange("p k t -> p (k t)"),
                                                ALU.subtract).then_inc(xlo_d, 1)

                def group(g, more):
                    add_q(g, L0_QG, 0, range(0, 2), 0)
                    dve.wait_ge(h_mm, g + 1)
                    nc.vector.tensor_tensor(h_own[:], ps[:, HBANK, 0:GT].rearrange("p (b s) -> p b s", b=GB),
                                            own[:].to_broadcast([P, GB, SEQ]), ALU.mult).then_inc(h_own_d, 1)
                    add_q(g, L0_QG, 0, range(2, 3), 0)
                    dve.wait_ge(h_hi_d, g + 1)
                    nc.vector.tensor_tensor(h_lo[:], h_own[:].rearrange("p b s -> p (b s)"), h_hi[:].bitcast(F32),
                                            ALU.subtract).then_inc(h_lo_d, 1)
                    add_q(g, L0_QG, 0, range(3, 10), 0)
                    if more:
                        split_x(g + 1)
                    add_q(g, L0_QG, 0, range(10, L0_QG), 0)

                split_x(0)
                dve.wait_ge(dve_s, 5)
                dve.wait_ge(cst, 7)
                nc.vector.tensor_tensor(lang_bias[:], lang_tt[:].to_broadcast([P, TT, NE]),
                                        iota8[:].rearrange("p (a e) -> p a e", a=1).to_broadcast([P, TT, NE]),
                                        ALU.is_equal).then_inc(dve_s, 1)
                dve.wait_ge(dve_s, 6)
                nc.vector.tensor_scalar(lang_bias[:], lang_bias[:], LANG_BIAS, None, ALU.mult).then_inc(dve_s, 1)
                dve.wait_ge(w3_ld, 16)
                nc.vector.tensor_scalar(w3_sum[:], w3_sum[:], s0[:, 0:1], None, ALU.add).then_inc(w3_s0, 1)
                dve.wait_ge(w3_s0, 1)
                with dve.Fori(0, NG - 1) as g:
                    group(g, True)
                group(NG - 1, False)


        with ExitStack() as l1:
            w_hi = sb("w1_hi", [P, KT, AW + D], F32R, l1)
            w_lo = sb("w1_lo", [P, KT, AW + D], F32R, l1)
            b1_hi = sb("b1_hi", [P, D], F32R, l1)
            b1_lo = sb("b1_lo", [P, D], F32R, l1)
            x1_hi = sb("x1_hi", [P, 2, KT, P], F32R, l1)
            x1_lo = sb("x1_lo", [P, 2, KT, P], F32R, l1)
            x1_hi_d, x1_lo_d = sem("x1_hi_d"), sem("x1_lo_d")
            prep1.w_hi, prep1.w_lo = w_hi, w_lo

            def split_x1_hi(it, d):
                if not (isinstance(it, int) and it == 0 and d == 0):
                    nc.scalar.wait_ge(base_mm, it * 2 + d)
                nc.scalar.activation(x1_hi[:, d, :, :], act[:, :, ds(it * 2 * P + d * P, P)], ACT.Copy)\
                  .then_inc(x1_hi_d, 1)

            def split_x1_lo(eng, it, d):
                eng.wait_ge(x1_hi_d, it * 2 + (d + 1))
                eng.tensor_tensor(x1_lo[:, d, :, :], act[:, :, ds(it * 2 * P + d * P, P)],
                                  x1_hi[:, d, :, :].bitcast(F32), ALU.subtract).then_inc(x1_lo_d, 1)

            with ExitStack() as ph:
                st_a = sb("st_a", [P, D], F32, ph)
                st_b = sb("st_b", [P, NE, KT, R], F32, ph)
                st_rb = sb("st_rb", [P, D], F32, ph)
                b_by_j = st_rb[:].rearrange("p (j e r) -> p j e r", j=KT, e=NE)
                SEQ_A, SEQ_R, SEQ_B = KT, KT + 1, KT + 2
                a_ld, r_ld, b_ld = sem("a_ld"), sem("r_ld"), sem("b_ld")
                r_zero, b_perm = sem("r_zero"), sem("b_perm")
                block = ph.enter_context(nc.Block())

                @block.sync
                def _(sp):
                    for n in range(ST, KT):
                        prep1.load(sp, n)
                    sp.dma_start(st_a[:], A1.rearrange("e r n -> (e r) n")).then_inc(a_ld, 16)
                    sp.wait_ge(r_zero, 1)
                    sp.dma_start(st_rb[0:NE, :], Wr).then_inc(r_ld, 16)
                    sp.dma_start(st_b[:].rearrange("p e j r -> p e (j r)"),
                                 B1.rearrange("e (p j) r -> p e (j r)", j=KT)).then_inc(b_ld, 16)
                    for b in range(RING):
                        sp.wait_ge(prep1.tp, KT - ST + b + 1)
                        load_q(sp, b, L0_Q // RING, 0)

                @block.gpsimd
                def _(pool):
                    prep1.pool(pool)

                @block.scalar
                def _(act_e):
                    prep1.scalar(act_e)
                    act_e.wait_ge(prep1.tp, SEQ_A + 1)
                    nc.scalar.activation(w_hi[:, :, 0:ER], tiles(0), ACT.Copy).then_inc(prep1.hi, 1)
                    act_e.wait_ge(prep1.tp, SEQ_R + 1)
                    act_e.wait_ge(b_ld, 16)
                    nc.scalar.activation(b_by_j, st_b[:].rearrange("p e j r -> p j e r"), ACT.Copy).then_inc(b_perm, 1)
                    nc.scalar.activation(w_hi[:, :, ER:AW], tiles(2)[:, :, 0:NE], ACT.Copy).then_inc(prep1.hi, 1)
                    split_x1_hi(0, 0)
                    act_e.wait_ge(prep1.tp, SEQ_B + 1)
                    nc.scalar.activation(b1_hi[:].rearrange("q (p j) -> q j p", j=KT), tiles(4), ACT.Copy,
                                         scale=SCALING).then_inc(prep1.hi, 1)

                @block.tensor
                def _(pe):
                    prep1.tensor(pe)
                    for seq, stage_, ld, pair in ((SEQ_A, st_a, a_ld, 0), (SEQ_R, st_rb, r_ld, 1)):
                        pe.wait_ge(ld, 16)
                        pe.wait_ge(prep1.lo, seq + 1)
                        prep1.to_banks(pair, lambda k: stage_[:, k * P:(k + 1) * P])
                    pe.wait_ge(b_perm, 1)
                    pe.wait_ge(prep1.lo, SEQ_B + 1)
                    prep1.to_banks(2, lambda j: b_by_j[:, j, :, :].rearrange("p e r -> p (e r)"))

                @block.vector
                def _(dve):
                    nc.vector.memset(st_rb[:], 0.0).then_inc(r_zero, 1)
                    prep1.vector(dve)
                    dve.wait_ge(prep1.hi, SEQ_A + 1)
                    nc.vector.tensor_tensor(w_lo[:, :, 0:ER], tiles(0), w_hi[:, :, 0:ER].bitcast(F32),
                                            ALU.subtract).then_inc(prep1.lo, 1)
                    dve.wait_ge(prep1.hi, SEQ_R + 1)
                    nc.vector.tensor_tensor(w_lo[:, :, ER:AW], tiles(2)[:, :, 0:NE],
                                            w_hi[:, :, ER:AW].bitcast(F32), ALU.subtract).then_inc(prep1.lo, 1)
                    split_x1_lo(dve, 0, 0)
                    dve.wait_ge(prep1.hi, SEQ_B + 1)
                    perm = "q (p j) -> q j p"
                    nc.vector.scalar_tensor_tensor(
                        out=b1_lo[:].rearrange(perm, j=KT), in0=tiles(4), scalar=SCALING,
                        in1=b1_hi[:].bitcast(F32).rearrange(perm, j=KT),
                        op0=ALU.mult, op1=ALU.subtract).then_inc(prep1.lo, 1)

            x2 = sb("x2", [P, D], F32, l1)
            w2_bd = sb("w2_bd", [P, 2, P], F32, l1)
            bias_bc = sb("bias_bc", [P, 2, 1, P], F32, l1)
            hg = sb("hg", [P, ER], F32, l1)
            hg_hi = sb("hg_hi", [P, P], F32R, l1)
            hg_lo = sb("hg_lo", [P, P], F32R, l1)
            logit = sb("logit", [P, NE], F32, l1)
            top = sb("top", [P, NE], F32, l1)
            top_i = sb("top_i", [P, NE], U32, l1)
            top_f = sb("top_f", [P, 2], F32, l1)
            gap = sb("gap", [P, 1], F32, l1)
            e_gap = sb("e_gap", [P, 1], F32, l1)
            e_sum = sb("e_sum", [P, 1], F32, l1)
            g_w = sb("g_w", [P, 2], F32, l1)
            g_one = sb("g_one", [P, 2, NE], F32, l1)
            gate = sb("gate", [P, NE, 1], F32, l1)
            CUTS = (0, 388, 776, AW + D)
            PIECES = [(CUTS[i], CUTS[i + 1], max(CUTS[i], AW)) for i in range(3)]
            OUT2 = 6
            h1_mm, hgt, y1_mm, l2_mm = (sem(n) for n in ("h1_mm", "hgt", "y1_mm", "l2_mm"))
            gs = sem("gs")
            GS = 11
            gap_exp, hg_hi_d, hg_lo_d = sem("gap_exp"), sem("hg_hi_d"), sem("hg_lo_d")
            prep3 = Prep("w3", w3_upper, stage, HB, None, None, prep_lo[2])
            w2_zero, w2_ld = sem("w2_zero"), [sem(f"w2_ld{d}") for d in range(2)]
            w2_d = sem("w2_d")
            block = l1.enter_context(nc.Block())

            @block.sync
            def _(sp):
                per, n0 = 2 * L1_QT, L0_Q
                last = TT // 2 - 1
                with sp.Fori(0, L1_UP - 1) as it:
                    stream_q(sp, it, per, n0, range(per), 0)
                stream_q(sp, L1_UP - 1, per, n0, range(per - RING), 0)
                for b in range(HB):
                    sp.wait_ge(sum_done, UP_Q + b + 1)
                    sp.dma_start(w3_upper[b * P:(b + 1) * P, :], w3_sum[:, b, :]).then_inc(up_st[b], 16)
                    stream_q(sp, L1_UP - 1, per, n0, [per - RING + b], 1)
                with sp.Fori(L1_UP, last) as it:
                    stream_q(sp, it, per, n0, range(per), 1)
                stream_q(sp, last, per, n0, range(per - RING), 1)
                for b in range(ST):
                    sp.wait_ge(up_st[b], 16)
                    sp.wait_ge(sum_done, L0_Q + TT * L1_QT + b + 1)
                    prep3.load(sp, b)

            @block.gpsimd
            def _(pool):
                def load(it, d):
                    for c in range(2):
                        s = pool.value_load(subj_row[0:1, ds(it * 4 + (2 * d + c), 1)], min_val=0,
                                            max_val=w2.shape[0] - 1)
                        part = slice(c * SEQ, (c + 1) * SEQ)
                        pool.dma_start(w2_bd[part, d, part], w2[ds(s, 1), :, :].rearrange("a c n -> (a c) n"))\
                            .then_inc(w2_ld[d], 16)
                        pool.dma_start(bias_bc[:, d, 0, part],
                                       bias2[ds(s, 1), :, :].rearrange("a b n -> (a b) n").to_broadcast([P, SEQ]))\
                            .then_inc(w2_ld[d], 16)

                def tile(it, d):
                    pool.wait_ge(w2_ld[d], it * 64 + 64)
                    nc.gpsimd.tensor_tensor(w2_bd[:, d, :], w2_bd[:, d, :], ident[:], ALU.add).then_inc(w2_d, 1)

                def reload(it, d):
                    pool.wait_ge(x3_out, it * 2 + d)
                    load(it, d)

                nc.gpsimd.memset(w2_bd[:], 0.0).then_inc(w2_zero, 1)
                pool.wait_ge(w2_zero, 1)
                load(0, 0)
                load(0, 1)
                split_x1_lo(pool, 0, 1)
                tile(0, 0)
                tile(0, 1)
                split_x1_lo(pool, 1, 0)
                last = TT // 2 - 1
                with pool.Fori(1, last) as it:
                    reload(it, 0)
                    split_x1_lo(pool, it, 1)
                    tile(it, 0)
                    reload(it, 1)
                    split_x1_lo(pool, it + 1, 0)
                    tile(it, 1)
                reload(last, 0)
                split_x1_lo(pool, last, 1)
                tile(last, 0)
                reload(last, 1)
                tile(last, 1)

            @block.scalar
            def _(act_e):
                def tile(it, d, nxt):
                    n1 = d + 1
                    if nxt:
                        split_x1_hi(*nxt)
                    act_e.wait_ge(gs, it * (2 * GS) + (d * GS + 5))
                    nc.scalar.activation(e_gap[:], gap[:], ACT.Exp).then_inc(gap_exp, 1)
                    act_e.wait_ge(hgt, it * 2 + n1)
                    nc.scalar.activation(hg_hi[:], ps[:, OUT2, 0:P], ACT.Copy).then_inc(hg_hi_d, 1)
                    act_e.wait_ge(y1_mm, it * 2 + n1)
                    for i, (c0, c1, f) in enumerate(PIECES):
                        piece = nc.scalar.activation(x2[:, f - AW:c1 - AW], ps[:, 3 * d + i, f - c0:c1 - c0], ACT.Copy)
                    piece.then_inc(x2_d, 1)

                with act_e.Fori(0, TT // 2 - 1) as it:
                    tile(it, 0, (it, 1))
                    tile(it, 1, (it + 1, 0))
                tile(TT // 2 - 1, 0, (TT // 2 - 1, 1))
                tile(TT // 2 - 1, 1, None)

            @block.tensor
            def _(pe):
                def l2(it, d):
                    n1 = d + 1
                    pe.wait_ge(x2_d, it * 2 + (n1 + 2))
                    pe.wait_ge(w2_d, it * 2 + n1)
                    pe.wait_ge(x3_out, it * 2 + n1)
                    for k in range(KT):
                        cols = slice(k * P, (k + 1) * P)
                        last = nc.tensor.matmul(banks(OUT2)[:, cols], x2[:, cols], w2_bd[:, d, :],
                                                start=True, stop=True)
                    last.then_inc(l2_mm, 1)

                def tile(it, d, prev):
                    n1 = d + 1
                    pe.wait_ge(x1_lo_d, it * 2 + n1)
                    xh, xl = x1_hi[:, d, :, :], x1_lo[:, d, :, :]
                    pe.wait_ge(x2_d, it * 2 + n1)
                    for i, (c0, c1, f) in enumerate(PIECES):
                        if i == 2 and prev:
                            l2(*prev)
                        for k in range(KT):
                            for n, (a, b) in enumerate(((xh, w_hi), (xl, w_hi), (xh, w_lo))):
                                last = nc.tensor.matmul(ps[:, 3 * d + i, 0:c1 - c0], a[:, k, :], b[:, k, c0:c1],
                                                        start=(k == 0 and n == 0),
                                                        stop=(i == 0 and k == KT - 1 and n == 2))
                            if i == 2 and k == 5:
                                pe.wait_ge(gs, it * (2 * GS) + (d + 1) * GS)
                                pe.wait_ge(x3_out, it * 2 + n1)
                                nc.tensor.transpose(ps[:, OUT2, 0:P], hg[:], ident[:]).then_inc(hgt, 1)
                        if i == 0:
                            last.then_inc(h1_mm, 1)
                    last.then_inc(base_mm, 1)
                    pe.wait_ge(hg_lo_d, it * 2 + n1)
                    for i, (c0, c1, f) in enumerate(PIECES):
                        for n, (a, b) in enumerate(((hg_hi, b1_hi), (hg_lo, b1_hi), (hg_hi, b1_lo))):
                            last = nc.tensor.matmul(ps[:, 3 * d + i, f - c0:c1 - c0], a[:], b[:, f - AW:c1 - AW],
                                                    start=False, stop=(n == 2), skip_group_check=(i == 0))
                    last.then_inc(y1_mm, 1)

                tile(0, 0, None)
                tile(0, 1, (0, 0))
                with pe.Fori(1, TT // 2) as it:
                    tile(it, 0, (it - 1, 1))
                    tile(it, 1, (it, 0))
                l2(TT // 2 - 1, 1)

            @block.vector
            def _(dve):
                def out_x3(it, d):
                    dve.wait_ge(l2_mm, it * 2 + (d + 1))
                    nc.vector.tensor_tensor(act[:, :, ds(it * 2 * P + d * P, P)], tiles(OUT2),
                                            bias_bc[:, d, :, :].to_broadcast([P, KT, P]), ALU.add).then_inc(x3_out, 1)

                def gating(it, d, add):
                    base = it * (2 * GS) + d * GS
                    step = lambda n: dve.wait_ge(gs, base + n)
                    dve.wait_ge(h1_mm, it * 2 + (d + 1))
                    nc.vector.tensor_tensor(logit[:], ps[:, 3 * d, ER:AW],
                                            lang_bias[:, ds(it * 2 + d, 1), :].rearrange("p a e -> p (a e)"),
                                            ALU.add).then_inc(gs, 1)
                    step(1)
                    add(0)
                    nc.vector.max(top[:], logit[:]).then_inc(gs, 1)
                    step(2)
                    add(1)
                    nc.vector.max_index(top_i[:], top[:], logit[:]).then_inc(gs, 1)
                    step(3)
                    nc.vector.tensor_copy(top_f[:], top_i[:, 0:2]).then_inc(gs, 1)
                    nc.vector.tensor_tensor(gap[:], top[:, 1:2], top[:, 0:1], ALU.subtract).then_inc(gs, 1)
                    dve.wait_ge(gap_exp, it * 2 + (d + 1))
                    nc.vector.tensor_scalar(e_sum[:], e_gap[:], 1.0, None, ALU.add).then_inc(gs, 1)
                    step(6)
                    nc.vector.reciprocal(g_w[:, 0:1], e_sum[:]).then_inc(gs, 1)
                    step(7)
                    nc.vector.tensor_tensor(g_w[:, 1:2], g_w[:, 0:1], e_gap[:], ALU.mult).then_inc(gs, 1)
                    step(8)
                    for i in range(2):
                        last = nc.vector.tensor_scalar(g_one[:, i, :], iota8[:], top_f[:, i:i + 1], g_w[:, i:i + 1],
                                                       ALU.is_equal, ALU.mult)
                    last.then_inc(gs, 1)
                    step(9)
                    nc.vector.tensor_tensor(gate[:, :, 0], g_one[:, 0, :], g_one[:, 1, :], ALU.add).then_inc(gs, 1)
                    step(10)
                    nc.vector.tensor_tensor(hg[:].rearrange("p (e r) -> p e r", e=NE),
                                            ps[:, 3 * d, 0:ER].rearrange("p (e r) -> p e r", e=NE),
                                            gate[:].to_broadcast([P, NE, R]), ALU.mult).then_inc(gs, 1)

                def tile(it, d, prev, half):
                    def add(a, b):
                        if isinstance(it, int) and it == L1_UP:
                            begin = [j for j in range(d * L1_QT + a, d * L1_QT + b) if j < HB]
                            for j in begin:
                                dve.wait_ge(ring_ld[j], 16 * (UP_Q // RING + 1))
                                dve.wait_ge(up_st[j], 16)
                                nc.vector.tensor_scalar(w3_sum[:, j, :], ring[:, j, :], coef[:, 0:1], None, ALU.mult)\
                                  .then_inc(sum_done, 1)
                            a += len(begin)
                        add_q(it, 2 * L1_QT, L0_Q, range(d * L1_QT + a, d * L1_QT + b), half)

                    add(0, 3)
                    gating(it, d, lambda j: add(3 + j, 4 + j))
                    if prev:
                        out_x3(*prev)
                    add(5, 6)
                    dve.wait_ge(hg_hi_d, it * 2 + (d + 1))
                    nc.vector.tensor_tensor(hg_lo[:], ps[:, OUT2, 0:P], hg_hi[:].bitcast(F32), ALU.subtract)\
                      .then_inc(hg_lo_d, 1)
                    add(6, 8)

                def pair(it, half):
                    tile(it, 0, (it - 1, 1), half)
                    tile(it, 1, (it, 0), half)

                tile(0, 0, None, 0)
                tile(0, 1, (0, 0), 0)
                with dve.Fori(1, L1_UP) as it:
                    pair(it, 0)
                pair(L1_UP, 1)
                with dve.Fori(L1_UP + 1, TT // 2) as it:
                    pair(it, 1)
                out_x3(TT // 2 - 1, 1)

        with ExitStack() as l3:
            w_hi = sb("w3_hi", [P, KT, D], F32R, l3)
            w_lo = sb("w3_lo", [P, KT, D], F32R, l3)
            b3_bc = sb("b3_bc", [P, D], F32, l3)
            x3_hi = sb("x3_hi", [P, 2, KT, P], F32R, l3)
            x3_lo = sb("x3_lo", [P, 2, KT, P], F32R, l3)
            y_sb = sb("y_sb", [P, 2, NB], F32, l3)
            st_low = sb("st_low", [P, HB, D], F32, l3)
            bq_i = st_low[0:NQ, 0, :].bitcast(I32)
            bq_f = y_sb[0:NQ, :, :].rearrange("p a n -> p (a n)")
            sc_col = sb("sc_col", [NQ, 2], F32, l3)
            cb = sb("cb", [NQ, 1], F32, l3)
            cb_bc = sb("cb_bc", [NQ, P], F32, l3)
            ones = sb("ones", [NQ, P], F32, l3)
            prep3.w_hi, prep3.w_lo = w_hi, w_lo
            b3_ld, b3_s, b3_mm, bq_cv, b3_out = (sem(n) for n in ("b3_ld", "b3_s", "b3_mm", "bq_cv", "b3_out"))
            x3_hi_d, x3_lo_d, y3_mm = sem("x3_hi_d"), sem("x3_lo_d"), sem("y3_mm")
            y3_st = [sem(f"y3_st{d}") for d in range(2)]
            low_ld, low_w = sem("low_ld"), sem("low_w")
            low_id, low_tp, low_hi, low_lo = (sem(n) for n in ("low_id", "low_tp", "low_hi", "low_lo"))
            PER, N0 = 2 * L3_QT, L0_Q + TT * L1_QT
            ITS = TT // 2
            LOW_BANKS = (2, 4, 6, 2)
            block = l3.enter_context(nc.Block())

            @block.sync
            def _(sp):
                def store(it, d, half):
                    sp.wait_ge(y3_out, it * 2 + (half * TT + d + 3))
                    sp.dma_start(y_rows[ds(it * 2 * P + d * P, P), half * NB:(half + 1) * NB], y_sb[:, d, :])\
                      .then_inc(y3_st[d], 16)

                sp.dma_start(sc_col[:, 0:1], scale.rearrange("(n a) -> n a", a=1)).then_inc(b3_ld, 16)
                sp.dma_start(sc_col[:, 1:2], bscale.rearrange("(n a) -> n a", a=1)).then_inc(b3_ld, 16)
                sp.dma_start(bq_i, bq).then_inc(b3_ld, 16)
                sp.dma_start(b3_bc[:], row(b3).to_broadcast([P, D])).then_inc(b3_ld, 16)
                for b in range(HB):
                    sp.wait_ge(prep3.tp, b + 1)
                    load_q(sp, b, (N0 - UP_Q) // RING, 1)
                sp.wait_ge(bq_cv, 1)
                sp.dma_start(st_low[:], W3[HALF:D, :].rearrange("(b p) n -> p b n", p=P)).then_inc(low_ld, 16)
                with sp.Fori(0, ITS - 1) as it:
                    for d in range(2):
                        stream_q(sp, it, PER, N0, range(d * L3_QT, (d + 1) * L3_QT), 1)
                        store(it, d, 0)
                for d in range(2):
                    store(ITS - 1, d, 0)
                with sp.Fori(0, ITS) as it:
                    for d in range(2):
                        store(it, d, 1)
                for d in range(2):
                    sp.wait_ge(y3_st[d], 2 * 16 * ITS)

            @block.gpsimd
            def _(pool):
                prep3.pool(pool)
                for b in range(HB):
                    pool.wait_ge(sum_done, 2 * UP_Q + RING - HB + b + 1)
                    diag = w3_sum[:, b, (HB + b) * P:(HB + b + 1) * P]
                    nc.gpsimd.tensor_tensor(diag, diag, ident[:], ALU.add).then_inc(low_id, 1)

            @block.scalar
            def _(act_e):
                def split(it, d, half):
                    if not (isinstance(it, int) and it == 0 and half == 0):
                        act_e.wait_ge(y3_mm, it * 2 + (half * TT + d - 1))
                    nc.scalar.activation(x3_hi[:, d, :, :], act[:, :, ds(it * 2 * P + d * P, P)], ACT.Copy)\
                      .then_inc(x3_hi_d, 1)

                prep3.scalar(act_e)
                split(0, 0, 0)
                act_e.wait_ge(b3_ld, 64)
                nc.scalar.activation(bq_f, bq_i, ACT.Copy).then_inc(bq_cv, 1)
                split(0, 1, 0)
                with act_e.Fori(1, ITS) as it:
                    for d in range(2):
                        split(it, d, 0)
                for d in range(2):
                    split(0, d, 1)
                for b in range(HB):
                    act_e.wait_ge(low_tp, b + 1)
                    nc.scalar.activation(w_hi[:, :, (HB + b) * P:(HB + b + 1) * P], tiles(LOW_BANKS[b]), ACT.Copy)\
                      .then_inc(low_hi, 1)
                with act_e.Fori(1, ITS) as it:
                    for d in range(2):
                        split(it, d, 1)

            @block.tensor
            def _(pe):
                def half_of_l3(half):
                    with pe.Fori(0, ITS) as it:
                        for d in range(2):
                            pe.wait_ge(x3_lo_d, it * 2 + (half * TT + d + 1))
                            pe.wait_ge(y3_out, it * 2 + (half * TT + d + 1))
                            xh, xl = x3_hi[:, d, :, :], x3_lo[:, d, :, :]
                            cols = slice(half * NB, (half + 1) * NB)
                            for k in range(KT):
                                for n, (a, b) in enumerate(((xh, w_hi), (xl, w_hi), (xh, w_lo))):
                                    last = nc.tensor.matmul(ps[:, d, :], a[:, k, :], b[:, k, cols],
                                                            start=(k == 0 and n == 0), stop=(k == KT - 1 and n == 2))
                            last.then_inc(y3_mm, 1)

                prep3.tensor(pe)
                pe.wait_ge(b3_s, 3)
                pe.wait_ge(bq_cv, 1)
                for half in range(2):
                    pe.wait_ge(prep3.lo, ST + 2 * (half + 1))
                    cols = slice(half * NB, (half + 1) * NB)
                    last = nc.tensor.matmul(ps[:, 2 + half, :], cb_bc[:], bq_f[:, cols], start=True, stop=True)
                last.then_inc(b3_mm, 1)
                half_of_l3(0)
                for b in range(HB):
                    pe.wait_ge(low_id, b + 1)
                    if b == 3:
                        pe.wait_ge(low_lo, 1)
                    for k in range(KT):
                        last = nc.tensor.transpose(banks(LOW_BANKS[b])[:, k * P:(k + 1) * P],
                                                   w3_sum[:, b, k * P:(k + 1) * P], ident[:])
                    last.then_inc(low_tp, 1)
                pe.wait_ge(low_lo, HB)
                half_of_l3(1)

            @block.vector
            def _(dve):
                def split(it, d, half):
                    dve.wait_ge(x3_hi_d, it * 2 + (half * TT + d + 1))
                    nc.vector.tensor_tensor(x3_lo[:, d, :, :], act[:, :, ds(it * 2 * P + d * P, P)],
                                            x3_hi[:, d, :, :].bitcast(F32), ALU.subtract).then_inc(x3_lo_d, 1)

                def out(it, d, half):
                    dve.wait_ge(y3_mm, it * 2 + (half * TT + d + 1))
                    if not (isinstance(it, int) and it == 0 and half == 0):
                        dve.wait_ge(y3_st[d], it * 16 + 16 * half * ITS)
                    nc.vector.tensor_tensor(y_sb[:, d, :], ps[:, d, :], b3_bc[:, half * NB:(half + 1) * NB],
                                            ALU.add).then_inc(y3_out, 1)

                def tile(it, d, nxt, low=False):
                    split(*nxt)
                    if low:
                        dve.wait_ge(low_ld, 16)
                        for b in (2 * d, 2 * d + 1):
                            dve.wait_ge(sum_done, N0 + RING + 2 * d)
                            nc.vector.scalar_tensor_tensor(
                                out=w3_sum[:, b, :], in0=st_low[:, b, :], scalar=s0[:, 0:1], in1=w3_sum[:, b, :],
                                op0=ALU.add, op1=ALU.add).then_inc(low_w, 1)
                        dve.wait_ge(low_w, 2 * d + 2)
                    add_q(it, PER, N0, range(d * L3_QT, (d + 1) * L3_QT), 1)
                    out(it, d, 0)

                nc.vector.memset(ones[:], 1.0).then_inc(b3_s, 1)
                prep3.vector(dve)
                split(0, 0, 0)
                dve.wait_ge(b3_ld, 64)
                nc.vector.tensor_tensor(cb[:], sc_col[:, 0:1], sc_col[:, 1:2], ALU.mult).then_inc(b3_s, 1)
                dve.wait_ge(b3_s, 2)
                nc.vector.tensor_scalar(cb_bc[:], ones[:], cb[:, 0:1], None, ALU.mult).then_inc(b3_s, 1)
                dve.wait_ge(b3_mm, 1)
                nc.vector.scalar_tensor_tensor(out=b3_bc[:], in0=banks(2), scalar=s0[:, 0:1], in1=b3_bc[:],
                                               op0=ALU.add, op1=ALU.add).then_inc(b3_out, 1)
                dve.wait_ge(b3_out, 1)
                LAST = ITS - 1
                tile(0, 0, (0, 1, 0), low=True)
                tile(0, 1, (1, 0, 0), low=True)
                with dve.Fori(1, LAST) as it:
                    tile(it, 0, (it, 1, 0))
                    tile(it, 1, (it + 1, 0, 0))
                tile(LAST, 0, (LAST, 1, 0))
                tile(LAST, 1, (0, 0, 1))
                for b in range(HB):
                    dve.wait_ge(low_hi, b + 1)
                    o = slice((HB + b) * P, (HB + b + 1) * P)
                    nc.vector.tensor_tensor(w_lo[:, :, o], tiles(LOW_BANKS[b]), w_hi[:, :, o].bitcast(F32),
                                            ALU.subtract).then_inc(low_lo, 1)
                split(0, 1, 1)
                out(0, 0, 1)
                with dve.Fori(1, ITS) as it:
                    split(it, 0, 1)
                    out(it - 1, 1, 1)
                    split(it, 1, 1)
                    out(it, 0, 1)
                out(ITS - 1, 1, 1)


_INS = ["x", "condB_scale", "condB_wscale", "condB_bscale", "_lenS", "itok_B_0_23", "itok_B_0_7",
        "itok_B_0_31", "itok_Bx4096x4096_0_255", "itok_Bx4096_0_255", "L0_cond_W", "L0_cond_b",
        "L0_cond_lora_As", "L0_cond_lora_Bs", "L1_cond_W", "L1_cond_Wr", "L1_cond_A", "L1_cond_B",
        "L2_cond_weights", "L2_cond_biases", "L3_cond_weight", "L3_cond_bias"]


def kernel(**inputs):
    import numpy as np
    import concourse.bacc as bacc
    from concourse.bass_utils import run_bass_kernel_spmd

    nc = bacc.Bacc("TRN2", target_bir_lowering=False, num_devices=1)
    arrays, args = {}, []
    for name in _INS:
        a = np.ascontiguousarray(inputs[name])
        arrays[f"in_{name}"] = a
        args.append(nc.dram_tensor(f"in_{name}", a.shape, mybir.dt.from_np(a.dtype), kind="ExternalInput").ap())
    args.append(nc.dram_tensor("out", (BATCH, SEQ, D), F32, kind="ExternalOutput").ap())
    program(nc, *args)
    return run_bass_kernel_spmd(nc, [arrays], core_ids=[0]).results[0]["out"]
```

```python
from contextlib import ExitStack

import concourse.bass as bass
from concourse import mybir

F32 = mybir.dt.float32
F32R = mybir.dt.float32r
I32 = mybir.dt.int32
U32 = mybir.dt.uint32
ALU = mybir.AluOpType
ACT = mybir.ActivationFunctionType
AX_X = mybir.AxisListType.X
ds = bass.ds

P = 128
BATCH, SEQ, D = 32, 64, 1024
T = BATCH * SEQ
KT = D // P
TT = T // P
GT = 256
NG = T // GT
GB = GT // SEQ
R = 16
NE = 8
ER = NE * R
AW = ER + NE
NB = 512
NQ = 32
HB = 4
HALF = HB * P
RING = 4
UP_Q = NQ * HB
L0_QG = 12
L0_Q = NG * L0_QG
L0_N0 = -RING
L1_QT = 8
TAIL_Q = 2
L3_QT = 2
L1_UP = (UP_Q - L0_Q) // (2 * L1_QT)
LANG_BIAS = 5.0
SCALING = 2.0
assert L0_Q + L1_UP * 2 * L1_QT == UP_Q and L0_Q + TT * (L1_QT + L3_QT) == 2 * UP_Q


def program(nc, x, scale, wscale, bscale, len_s, slot_id, lang_id, subj_id, wq, bq,
            W0, b0, lora_A, lora_B, W1, Wr, A1, B1, w2, bias2, W3, b3, y):
    w3_upper = nc.dram_tensor("w3_upper", (HALF, D), F32, kind="Internal").ap()
    x_rows = x.rearrange("b s d -> (b s) d")
    y_rows = y.rearrange("b s d -> (b s) d")
    lora_A_v = lora_A.rearrange("s (p k) r -> s p (k r)", k=KT)
    row = lambda v: v.rearrange("(a n) -> a n", a=1)

    with ExitStack() as ctx:
        def sb(name, shape, dt=F32, where=ctx):
            return where.enter_context(nc.sbuf_tensor(name, shape, dt))

        def sem(name):
            return ctx.enter_context(nc.semaphore(name))

        ident = sb("ident", [P, P])
        act = sb("act", [P, KT, T])
        w3_sum = sb("w3_sum", [P, HB, D])
        ring = sb("ring", [P, RING, D], I32)
        coef = sb("coef", [P, NQ])
        s0 = sb("s0", [P, 1])
        b0_col = sb("b0_col", [P, KT])
        lang_bias = sb("lang_bias", [P, TT, NE])
        iota8 = sb("iota8", [P, NE])
        subj_row = sb("subj_row", [1, BATCH], I32)
        slot_row = sb("slot_row", [1, BATCH], I32)
        own = sb("own", [P, GB, 1])
        w_hi = sb("w_hi", [P, KT, AW + D], F32R)
        w_lo = sb("w_lo", [P, KT, AW + D], F32R)
        with ExitStack() as place:
            B_raw = sb("B_raw", [P, D], F32, place)
            rows_in = sb("rows_in", [P, 2, D], F32, place)
        b1_lo = sb("b1_lo", [P, D], F32R)
        x2 = sb("x2", [P, D])
        b1_hi = sb("b1_hi", [P, D], F32R)
        x_hi = sb("x_hi", [P, KT * GT], F32R)
        x_lo = sb("x_lo", [P, KT * GT], F32R)
        ps = ctx.enter_context(nc.psum_tensor("ps", [P, 8, NB], F32))

        def banks(b):
            return ps[:, b:b + 2, :].rearrange("p b n -> p (b n)")

        def tiles(b):
            return ps[:, b:b + 2, :].rearrange("p b (k n) -> p (b k) n", n=P)

        ring_ld = [sem(f"ring_ld{s}") for s in range(RING)]
        sum_done = sem("sum_done")
        y_out = sem("y_out")
        x2_d = sem("x2_d")
        x3_out = sem("x3_out")
        y3_out = sem("y3_out")
        base_mm = sem("base_mm")
        begin_with = {sum_done: RING, y_out: 2, x2_d: 2, y3_out: 2, x3_out: 1, base_mm: 1}
        w3_ld = sem("w3_ld")
        up_st = [sem(f"up_st{b}") for b in range(HB)]

        def load_q(eng, block, expert, half):
            r0 = half * HALF + block * P
            eng.dma_start(ring[:, block, :], wq[ds(expert, 1), r0:r0 + P, :]
                          .rearrange("a p n -> p (a n)")).then_inc(ring_ld[block], 16)

        def stream_q(eng, it, per, n0, js, half):
            for j in js:
                eng.wait_ge(sum_done, it * per + (n0 + j + RING + 1))
                load_q(eng, j % RING, it * (per // RING) + (n0 - half * UP_Q + j + RING) // RING, half)

        def add_q(it, per, n0, js, half):
            for j in js:
                s = j % RING
                nc.vector.wait_ge(ring_ld[s], it * (4 * per) + 16 * ((n0 + j) // RING + 1))
                nc.vector.wait_ge(sum_done, it * per + (n0 + j + 1))
                expert = it * (per // RING) + (n0 - half * UP_Q + j) // RING
                nc.vector.scalar_tensor_tensor(
                    out=w3_sum[:, s, :], in0=ring[:, s, :], scalar=coef[:, ds(expert, 1)],
                    in1=w3_sum[:, s, :], op0=ALU.mult, op1=ALU.add).then_inc(sum_done, 1)

        class Prep:

            def __init__(self, name, rows, slots, strided=False):
                self.rows, self.slots, self.strided = rows, slots, strided
                self.ld = [sem(f"{name}_ld{d}") for d in range(slots)]
                self.ident = sem(f"{name}_ident")
                self.tp = sem(f"{name}_tp")
                self.hi = sem(f"{name}_hi")
                self.lo = sem(f"{name}_lo")

            def load(self, eng, i, src):
                part = slice(0, src.shape[0])
                eng.dma_start(self.rows[part, i % self.slots, :], src).then_inc(self.ld[i % self.slots], 16)

            def arrived(self, eng, i):
                eng.wait_ge(self.ld[i % self.slots], 16 * (i // self.slots + 1))

            def add_identity(self, eng, i, n):
                self.arrived(eng, i)
                diag = self.rows[:, i % self.slots, n * P:(n + 1) * P]
                nc.gpsimd.tensor_tensor(diag, diag, ident[:], ALU.add).then_inc(self.ident, 1)

            def transpose(self, i, pair):
                rows = self.rows[:, i % self.slots, :]
                for k in range(KT):
                    src = rows[:, k::KT] if self.strided else rows[:, k * P:(k + 1) * P]
                    last = nc.tensor.transpose(banks(2 * pair)[:, k * P:(k + 1) * P], src, ident[:])
                last.then_inc(self.tp, 1)

            def high(self, i, pair, c0, n=P):
                nc.scalar.wait_ge(self.tp, i + 1)
                nc.scalar.activation(w_hi[:, :, c0:c0 + n], tiles(2 * pair)[:, :, 0:n], ACT.Copy)\
                  .then_inc(self.hi, 1)

            def low(self, i, pair, c0, n=P):
                nc.vector.wait_ge(self.hi, i + 1)
                nc.vector.tensor_tensor(w_lo[:, :, c0:c0 + n], tiles(2 * pair)[:, :, 0:n],
                                        w_hi[:, :, c0:c0 + n].bitcast(F32), ALU.subtract).then_inc(self.lo, 1)

        stage = ring[:].bitcast(F32)

        x1_hi = x_hi[:].rearrange("p (d k t) -> p d k t", d=2, k=KT)
        x1_lo = x_lo[:].rearrange("p (d k t) -> p d k t", d=2, k=KT)
        x1_hi_d, x1_lo_d = sem("x1_hi_d"), sem("x1_lo_d")

        def split_x1_hi(it, d):
            if not (isinstance(it, int) and it == 0 and d == 0):
                nc.scalar.wait_ge(base_mm, it * 2 + d)
            nc.scalar.activation(x1_hi[:, d, :, :], act[:, :, ds(it * 2 * P + d * P, P)], ACT.Copy)\
              .then_inc(x1_hi_d, 1)

        def split_x1_lo(eng, it, d):
            eng.wait_ge(x1_hi_d, it * 2 + (d + 1))
            eng.tensor_tensor(x1_lo[:, d, :, :], act[:, :, ds(it * 2 * P + d * P, P)],
                              x1_hi[:, d, :, :].bitcast(F32), ALU.subtract).then_inc(x1_lo_d, 1)

        CUTS = (0, 388, 776, AW + D)
        PIECES = [(CUTS[i], CUTS[i + 1], max(CUTS[i], AW)) for i in range(3)]
        h1_mm = sem("h1_mm")

        h_own = sb("h_own", [P, GB, SEQ])
        hg = h_own[:].rearrange("p b s -> p (b s)")[:, 0:ER]
        logit = sb("logit", [P, NE], F32)
        top = sb("top", [P, NE], F32)
        top_i = sb("top_i", [P, NE], U32)
        top_f = sb("top_f", [P, 2], F32)
        gap = sb("gap", [P, 1], F32)
        e_gap = sb("e_gap", [P, 1], F32)
        e_sum = sb("e_sum", [P, 1], F32)
        g_w = sb("g_w", [P, 2], F32)
        g_one = sb("g_one", [P, 2, NE], F32)
        gate = sb("gate", [P, NE, 1], F32)
        gs = sem("gs")
        GS = 11
        gap_exp = sem("gap_exp")

        def exp_gap(it, d):
            nc.scalar.wait_ge(gs, it * (2 * GS) + (d * GS + 5))
            nc.scalar.activation(e_gap[:], gap[:], ACT.Exp).then_inc(gap_exp, 1)

        def gating(it, d, add):
            base = it * (2 * GS) + d * GS
            step = lambda n: nc.vector.wait_ge(gs, base + n)
            nc.vector.wait_ge(h1_mm, it * 2 + (d + 1))
            nc.vector.tensor_tensor(logit[:], ps[:, 3 * d, ER:AW],
                                    lang_bias[:, ds(it * 2 + d, 1), :].rearrange("p a e -> p (a e)"),
                                    ALU.add).then_inc(gs, 1)
            step(1)
            add(0)
            nc.vector.max(top[:], logit[:]).then_inc(gs, 1)
            step(2)
            add(1)
            nc.vector.max_index(top_i[:], top[:], logit[:]).then_inc(gs, 1)
            step(3)
            nc.vector.tensor_copy(top_f[:], top_i[:, 0:2]).then_inc(gs, 1)
            nc.vector.tensor_tensor(gap[:], top[:, 1:2], top[:, 0:1], ALU.subtract).then_inc(gs, 1)
            nc.vector.wait_ge(gap_exp, it * 2 + (d + 1))
            nc.vector.tensor_scalar(e_sum[:], e_gap[:], 1.0, None, ALU.add).then_inc(gs, 1)
            step(6)
            nc.vector.reciprocal(g_w[:, 0:1], e_sum[:]).then_inc(gs, 1)
            step(7)
            nc.vector.tensor_tensor(g_w[:, 1:2], g_w[:, 0:1], e_gap[:], ALU.mult).then_inc(gs, 1)
            step(8)
            for i in range(2):
                last = nc.vector.tensor_scalar(g_one[:, i, :], iota8[:], top_f[:, i:i + 1], g_w[:, i:i + 1],
                                               ALU.is_equal, ALU.mult)
            last.then_inc(gs, 1)
            step(9)
            nc.vector.tensor_tensor(gate[:, :, 0], g_one[:, 0, :], g_one[:, 1, :], ALU.add).then_inc(gs, 1)
            step(10)
            nc.vector.tensor_tensor(hg.rearrange("p (e r) -> p e r", e=NE),
                                    ps[:, 3 * d, 0:ER].rearrange("p (e r) -> p e r", e=NE),
                                    gate[:].to_broadcast([P, NE, R]), ALU.mult).then_inc(gs, 1)

        def l1_piece(d, i, ks=range(KT)):
            c0, c1, f = PIECES[i]
            xh, xl = x1_hi[:, d, :, :], x1_lo[:, d, :, :]
            for k in ks:
                for n, (a, b) in enumerate(((xh, w_hi), (xl, w_hi), (xh, w_lo))):
                    last = nc.tensor.matmul(ps[:, 3 * d + i, 0:c1 - c0], a[:, k, :], b[:, k, c0:c1],
                                            start=(k == 0 and n == 0),
                                            stop=(i == 0 and k == KT - 1 and n == 2))
            return last

        with ExitStack() as ph:
            A_raw = sb("A_raw", [P, GB, KT * R], F32, ph)
            xT_hi = x_hi[:].rearrange("p (k t) -> p k t", k=KT)
            xT_lo = x_lo[:].rearrange("p (k t) -> p k t", k=KT)
            A_hi = w_hi[:, :, 0:P]
            A_lo = w_lo[:, :, 0:P]
            B_st = sb("B_st", [P, D], F32R, ph)
            h_hi = sb("h_hi", [P, GT], F32R, ph)
            h_lo = sb("h_lo", [P, GT], F32R, ph)
            consts = h_own[:].rearrange("p b s -> p (b s)")
            scale_bc, wscale_bc, len_bc, len_f, lang_bc = (consts[:, n * NQ:(n + 1) * NQ] for n in range(5))
            len_bc, lang_bc = len_bc.bitcast(I32), lang_bc.bitcast(I32)
            lang_tt = sb("lang_tt", [P, TT, 1], F32, ph)
            same = sb("same", [P, 2 * GB], F32, ph)
            PAIRS = KT // 2
            HBANK = 6
            Y = [(4, 5, 7)[o % 3] for o in range(KT)]
            x_ld = [sem(f"x_ld{d}") for d in range(2)]
            A_ld, B_ld = sem("A_ld"), sem("B_ld")
            consts_ld, rows_ld = sem("consts_ld"), sem("rows_ld")
            len_d = sem("len_d")
            cst = sem("cst")
            dve_s = sem("dve_s")
            A_hi_d, A_lo_d, B_hi_d, B_lo_d = sem("A_hi_d"), sem("A_lo_d"), sem("B_hi_d"), sem("B_lo_d")
            xtp = sem("xtp")
            xhi_d, xlo_d = sem("xhi_d"), sem("xlo_d")
            x_used = sem("x_used")
            h_mm, h_own_d, h_hi_d, h_lo_d = sem("h_mm"), sem("h_own_d"), sem("h_hi_d"), sem("h_lo_d")
            w3_s0 = sem("w3_s0")
            y_mm = sem("y_mm")
            prep0 = Prep("w0", stage, RING, strided=True)
            PAIR0 = (2, 0, 1, 0, 1, 0, 1, 0)
            prep1 = Prep("w1", rows_in, 2)
            SEQ1 = ("A", 0, 1, 2, 3, 4, 5, 6, "R", 7, "B")
            PAIR1 = (0, 1, 0, 1, 0, 1, 0, 1, 3, 2, 3)
            ITEM_R, ITEM_B = SEQ1.index("R"), SEQ1.index("B")
            B1_raw = B_raw[:].rearrange("p (e j r) -> p e j r", e=NE, j=KT)
            b_by_j = rows_in[:, ITEM_B % 2, :].rearrange("p (j e r) -> p j e r", j=KT, e=NE)
            b1_ld, b_perm = sem("b1_ld"), sem("b_perm")
            LG = NG - 1
            ADDS1 = (1, 1, 2, 2, 2, 2, 2, 1, 3, 0)
            assert sum(ADDS1) == L0_QG + RING

            def low_A(eng, g):
                eng.wait_ge(A_hi_d, g + 1)
                raw = A_raw[:].rearrange("p b (k r) -> p k b r", k=KT)
                for copy in range(2):
                    cols = slice(copy * GB * R, (copy + 1) * GB * R)
                    hi = A_hi[:, :, cols].bitcast(F32).rearrange("p k (b r) -> p k b r", b=GB)
                    lo = A_lo[:, :, cols].rearrange("p k (b r) -> p k b r", b=GB)
                    last = eng.tensor_tensor(lo, raw, hi, ALU.subtract)
                last.then_inc(A_lo_d, 1)

            block = ph.enter_context(nc.Block())

            @block.sync
            def _(sp):
                def load_x(g):
                    for d in range(2):
                        sp.dma_start(rows_in[:, d, :], x_rows[ds(g * GT + d * P, P), :]).then_inc(x_ld[d], 16)

                def load_adapters(g):
                    for b in range(GB):
                        s = sp.value_load(slot_row[0:1, ds(g * GB + b, 1)], min_val=0, max_val=lora_A.shape[0] - 1)
                        sp.dma_start(A_raw[:, b, :], lora_A_v[ds(s, 1), :, :].rearrange("a p n -> p (a n)"))\
                          .then_inc(A_ld, 16)
                        for copy in range(2):
                            r0 = copy * GB * R + b * R
                            sp.dma_start(B_raw[r0:r0 + R, :], lora_B[ds(s, 1), :, :].rearrange("a r n -> (a r) n"))\
                              .then_inc(B_ld, 16)

                def load_w0(n):
                    if n >= RING:
                        sp.wait_ge(prep0.tp, n - RING + 1)
                    prep0.load(sp, n, W0[n * P:(n + 1) * P, :])

                load_x(0)
                for n in range(4):
                    load_w0(n)
                sp.wait_ge(rows_ld, 48)
                load_adapters(0)
                load_w0(4)
                load_w0(5)
                sp.dma_start(w3_sum[:], W3[0:HALF, :].rearrange("(b p) n -> p b n", p=P)).then_inc(w3_ld, 16)
                load_w0(6)
                load_w0(7)
                sp.wait_ge(xtp, PAIRS)
                load_x(1)
                sp.wait_ge(A_lo_d, 1)
                sp.wait_ge(B_lo_d, 1)
                load_adapters(1)
                for b in range(RING):
                    sp.wait_ge(prep0.tp, KT - RING + b + 1)
                    load_q(sp, b, 0, 0)
                stream_q(sp, 0, L0_QG, L0_N0, range(RING, 10), 0)
                sp.wait_ge(xtp, 2 * PAIRS)
                load_x(2)
                stream_q(sp, 0, L0_QG, L0_N0, range(10, L0_QG), 0)
                with sp.Fori(1, LG - 1) as g:
                    stream_q(sp, g, L0_QG, L0_N0, range(5), 0)
                    sp.wait_ge(A_lo_d, g + 1)
                    sp.wait_ge(B_lo_d, g + 1)
                    load_adapters(g + 1)
                    stream_q(sp, g, L0_QG, L0_N0, range(5, 10), 0)
                    sp.wait_ge(xtp, g * PAIRS + 2 * PAIRS)
                    load_x(g + 2)
                    stream_q(sp, g, L0_QG, L0_N0, range(10, L0_QG), 0)
                stream_q(sp, LG - 1, L0_QG, L0_N0, range(5), 0)
                sp.wait_ge(A_lo_d, LG)
                sp.wait_ge(B_lo_d, LG)
                load_adapters(LG)
                stream_q(sp, LG - 1, L0_QG, L0_N0, range(5, 10), 0)
                sp.wait_ge(xtp, NG * PAIRS)
                free_q = 0
                for i, what in enumerate(SEQ1):
                    if i >= 2:
                        sp.wait_ge(prep1.tp, i - 1)
                    if what == "A":
                        prep1.load(sp, i, A1.rearrange("e r n -> (e r) n"))
                    elif what == "R":
                        prep1.load(sp, i, Wr)
                    elif what != "B":
                        prep1.load(sp, i, W1[what * P:(what + 1) * P, :])
                    if i == 1:
                        stream_q(sp, LG - 1, L0_QG, L0_N0, range(10, L0_QG), 0)
                    if i >= 2:
                        more_q = ADDS1[i - 2]
                        stream_q(sp, LG, L0_QG, L0_N0, range(free_q, free_q + more_q), 0)
                        free_q += more_q
                    if i == 1:
                        sp.wait_ge(B_lo_d, NG)
                        sp.dma_start(B1_raw.rearrange("p e j r -> p e (j r)"),
                                     B1.rearrange("e (p j) r -> p e (j r)", j=KT)).then_inc(b1_ld, 16)
                stream_q(sp, LG, L0_QG, L0_N0, range(free_q, L0_QG + RING), 0)
                stream_q(sp, 0, 2 * L1_QT, L0_Q, range(TAIL_Q), 0)

            @block.gpsimd
            def _(pool):
                nc.gpsimd.memset(ident[:], 0.0).then_inc(cst, 1)
                pool.wait_ge(cst, 1)
                nc.gpsimd.affine_select(out=ident[:], in_=ident[:], compare_op=ALU.not_equal, fill=1.0, base=0,
                                        pattern=[[-1, P]], channel_multiplier=1).then_inc(cst, 1)
                for s, count in begin_with.items():
                    pool.sem_inc(s, count)
                nc.gpsimd.memset(same[:], SCALING).then_inc(cst, 1)
                pool.wait_ge(cst, 3)
                nc.gpsimd.affine_select(out=same[:], in_=same[:], compare_op=ALU.is_ge, fill=0.0, base=0,
                                        pattern=[[-R, 2 * GB]], channel_multiplier=1).then_inc(cst, 1)
                pool.wait_ge(cst, 4)
                nc.gpsimd.affine_select(out=same[:], in_=same[:], compare_op=ALU.is_ge, fill=0.0, base=R - 1,
                                        pattern=[[R, 2 * GB]], channel_multiplier=-1).then_inc(cst, 1)
                pool.wait_ge(cst, 5)
                nc.gpsimd.tensor_tensor(own[:, :, 0], same[:, 0:GB], same[:, GB:2 * GB], ALU.add).then_inc(cst, 1)
                nc.gpsimd.iota(iota8[:], pattern=[[1, NE]], base=0, channel_multiplier=0,
                               allow_small_or_imprecise_dtypes=True).then_inc(cst, 1)
                pool.wait_ge(rows_ld, 48)

                def split_B(g):
                    pool.wait_ge(A_lo_d, g + 1)
                    pool.wait_ge(B_hi_d, g + 1)
                    low = slice(GB * R, P)
                    nc.gpsimd.tensor_tensor(B_st[low, :], B_raw[low, :], B_st[low, :].bitcast(F32),
                                            ALU.subtract).then_inc(B_lo_d, 1)

                for n in range(4):
                    prep0.add_identity(pool, n, n)
                pool.wait_ge(prep0.ident, 4)
                split_B(0)
                pool.wait_ge(B_lo_d, 1)
                for n in range(4, KT):
                    prep0.add_identity(pool, n, n)
                with pool.Fori(0, NG - 1) as g:
                    pool.wait_ge(B_lo_d, g + 1)
                    low_A(pool, g + 1)
                    split_B(g + 1)
                pool.wait_ge(B_lo_d, NG)
                for i, what in enumerate(SEQ1):
                    if isinstance(what, int):
                        prep1.add_identity(pool, i, what)

            @block.scalar
            def _(act_e):
                act_e.dma_start(slot_row[:], row(slot_id)).then_inc(rows_ld, 16)
                act_e.dma_start(subj_row[:], row(subj_id)).then_inc(rows_ld, 16)
                with nc.allow_non_contiguous_dma(reason="1024 values of the bias, once"):
                    act_e.dma_start(b0_col[:], b0.rearrange("(k p) -> p k", p=P)).then_inc(rows_ld, 16)
                for dst, src in ((scale_bc, scale), (wscale_bc, wscale), (len_bc, len_s), (lang_bc, lang_id)):
                    act_e.dma_start(dst, row(src).to_broadcast([P, NQ])).then_inc(consts_ld, 16)

                def split_A(g):
                    act_e.wait_ge(A_ld, g * (16 * GB) + 16 * GB)
                    raw = A_raw[:].rearrange("p b (k r) -> p k b r", k=KT)
                    for copy in range(2):
                        cols = slice(copy * GB * R, (copy + 1) * GB * R)
                        last = nc.scalar.activation(A_hi[:, :, cols].rearrange("p k (b r) -> p k b r", b=GB),
                                                    raw, ACT.Copy)
                    last.then_inc(A_hi_d, 1)

                def split_B(g):
                    act_e.wait_ge(B_ld, g * (32 * GB) + 32 * GB)
                    nc.scalar.activation(B_st[:], B_raw[:], ACT.Copy).then_inc(B_hi_d, 1)

                def split_x(g):
                    for j in range(PAIRS):
                        act_e.wait_ge(xtp, g * PAIRS + (j + 1))
                        if not (isinstance(g, int) and g == 0):
                            act_e.wait_ge(x_used, (g - 1) * PAIRS + (j + 1))
                        nc.scalar.activation(xT_hi[:, 2 * j:2 * j + 2, :].rearrange("p k t -> p (k t)"),
                                             ps[:, j, :], ACT.Copy).then_inc(xhi_d, 1)

                def out(g, o):
                    act_e.wait_ge(y_mm, g * KT + (o + 1))
                    nc.scalar.activation(act[:, o, ds(g * GT, GT)], ps[:, Y[o], 0:GT], ACT.Identity,
                                         bias=b0_col[:, o:o + 1]).then_inc(y_out, 1)

                def split_h(g):
                    act_e.wait_ge(h_own_d, g + 1)
                    nc.scalar.activation(h_hi[:], h_own[:].rearrange("p b s -> p (b s)"), ACT.Copy)\
                      .then_inc(h_hi_d, 1)

                def end_of_group(g):
                    out(g, 5)
                    split_A(g + 1)
                    out(g, 6)
                    split_x(g + 1)
                    out(g, KT - 1)
                    split_B(g + 1)

                def w0_high(n):
                    prep0.high(n, PAIR0[n], AW + n * P)

                split_x(0)
                for n in range(2):
                    w0_high(n)
                act_e.wait_ge(consts_ld, 64)
                nc.scalar.activation(len_f, len_bc, ACT.Copy).then_inc(len_d, 1)
                w0_high(2)
                split_A(0)
                w0_high(3)
                split_B(0)
                split_h(0)
                w0_high(4)
                act_e.wait_ge(rows_ld, 48)
                out(0, 0)
                out(0, 1)
                for o in range(2, 5):
                    w0_high(o + 3)
                    out(0, o)
                end_of_group(0)
                with act_e.Fori(1, LG) as g:
                    split_h(g)
                    for o in range(5):
                        out(g, o)
                    end_of_group(g)

                def w1_high(i):
                    if i == ITEM_R:
                        prep1.high(i, PAIR1[i], ER, NE)
                        act_e.wait_ge(b1_ld, 16)
                        nc.scalar.activation(b_by_j, B1_raw.rearrange("p e j r -> p j e r"), ACT.Copy)\
                          .then_inc(b_perm, 1)
                    elif i == ITEM_B:
                        act_e.wait_ge(prep1.tp, i + 1)
                        nc.scalar.activation(b1_hi[:].rearrange("q (p j) -> q j p", j=KT), tiles(2 * PAIR1[i]),
                                             ACT.Copy, scale=SCALING).then_inc(prep1.hi, 1)
                    else:
                        prep1.high(i, PAIR1[i], 0 if i == 0 else AW + SEQ1[i] * P)

                split_h(LG)
                w1_high(0)
                w1_high(1)
                out(LG, 0)
                out(LG, 1)
                for o in range(2, KT - 1):
                    w1_high(o)
                    out(LG, o)
                w1_high(KT - 1)
                act_e.wait_ge(y_out, 2 + KT)
                act_e.wait_ge(x_used, LG * PAIRS + PAIRS // 2)
                split_x1_hi(0, 0)
                out(LG, KT - 1)
                w1_high(ITEM_R)
                exp_gap(0, 0)
                w1_high(ITEM_R + 1)
                w1_high(ITEM_B)

            @block.tensor
            def _(pe):
                pe.wait_ge(cst, 2)

                def transpose_x(g):
                    pe.wait_ge(x_ld[0], g * 16 + 16)
                    for k in range(KT):
                        x_tile(k, 0)
                    pe.wait_ge(x_ld[1], g * 16 + 16)
                    for k in range(KT):
                        last = x_tile(k, 1)
                        if k % 2:
                            last.then_inc(xtp, 1)

                def x_tile(k, d):
                    c = (k % 2) * GT + d * P
                    return nc.tensor.transpose(ps[:, k // 2, c:c + P], rows_in[:, d, k::KT], ident[:])

                def adapters(g):
                    pe.wait_ge(A_lo_d, g + 1)
                    for k in range(KT):
                        if k % 2 == 0:
                            pe.wait_ge(xlo_d, g * PAIRS + (k // 2 + 1))
                        for n, (a, b) in enumerate(((A_hi, xT_hi), (A_lo, xT_hi), (A_hi, xT_lo))):
                            last = nc.tensor.matmul(ps[:, HBANK, 0:GT], a[:, k, :], b[:, k, :],
                                                    start=(k == 0 and n == 0), stop=(k == KT - 1 and n == 2))
                    last.then_inc(h_mm, 1)

                def base(g, o):
                    pe.wait_ge(y_out, g * KT + (o + 1 if o < 2 else o))
                    cols = slice(AW + o * P, AW + (o + 1) * P)
                    for k in range(KT):
                        for n, (a, b) in enumerate(((w_hi, xT_hi), (w_lo, xT_hi), (w_hi, xT_lo))):
                            last = nc.tensor.matmul(ps[:, Y[o], 0:GT], a[:, k, cols], b[:, k, :],
                                                    start=(k == 0 and n == 0), stop=False)
                        if o == KT - 1 and k % 2:
                            last.then_inc(x_used, 1)

                def lora(o):
                    cols = slice(o * P, (o + 1) * P)
                    nc.tensor.matmul(ps[:, Y[o], 0:GT], B_st[:, cols], h_hi[:], start=False, stop=False)
                    nc.tensor.matmul(ps[:, Y[o], 0:GT], B_st[:, cols], h_lo[:], start=False, stop=True)\
                      .then_inc(y_mm, 1)

                def wait_h(g):
                    pe.wait_ge(h_lo_d, g + 1)
                    pe.wait_ge(B_lo_d, g + 1)

                def w0_transpose(n):
                    pe.wait_ge(prep0.ident, n + 1)
                    if n in (1, 2):
                        pe.wait_ge(xlo_d, 2 * n)
                    elif n > 2:
                        pe.wait_ge(prep0.lo, n - 1)
                    prep0.transpose(n, PAIR0[n])

                transpose_x(0)
                for n in range(3):
                    w0_transpose(n)
                pe.wait_ge(prep0.lo, 1)
                base(0, 0)
                w0_transpose(3)
                pe.wait_ge(prep0.lo, 2)
                base(0, 1)
                adapters(0)
                w0_transpose(4)
                wait_h(0)
                lora(0)
                lora(1)
                for o in range(2, KT):
                    if o + 3 < KT:
                        w0_transpose(o + 3)
                    pe.wait_ge(prep0.lo, o + 1)
                    base(0, o)
                    lora(o)
                    if o == 5:
                        pe.wait_ge(prep0.lo, KT)
                        transpose_x(1)
                with pe.Fori(1, LG) as g:
                    adapters(g)
                    base(g, 0)
                    base(g, 1)
                    wait_h(g)
                    lora(0)
                    lora(1)
                    for o in range(2, KT):
                        base(g, o)
                        lora(o)
                        if o == 4:
                            transpose_x(g + 1)

                def w1_transpose(i):
                    what, pair = SEQ1[i], PAIR1[i]
                    earlier = [j for j in range(i) if PAIR1[j] == pair]
                    if earlier:
                        pe.wait_ge(prep1.lo, earlier[-1] + 1)
                    elif pair >= 2:
                        pe.wait_ge(y_out, LG * KT + 2 + (6 if pair == 3 else KT))
                    if what == "R":
                        prep1.arrived(pe, i)
                        for k in range(KT):
                            last = nc.tensor.transpose(tiles(2 * pair)[:, k, 0:NE],
                                                       rows_in[0:NE, i % 2, k * P:(k + 1) * P], ident[0:NE, 0:NE])
                        last.then_inc(prep1.tp, 1)
                        return
                    if what == "A":
                        prep1.arrived(pe, i)
                    elif what == "B":
                        pe.wait_ge(b_perm, 1)
                    else:
                        pe.wait_ge(prep1.ident, what + 1)
                    prep1.transpose(i, pair)

                adapters(LG)
                base(LG, 0)
                w1_transpose(0)
                base(LG, 1)
                w1_transpose(1)
                wait_h(LG)
                lora(0)
                lora(1)
                for o in range(2, KT):
                    w1_transpose(o)
                    base(LG, o)
                    lora(o)
                w1_transpose(ITEM_R)
                pe.wait_ge(x1_lo_d, 1)
                pe.wait_ge(prep1.lo, ITEM_R + 1)
                l1_piece(0, 0).then_inc(h1_mm, 1)
                w1_transpose(ITEM_R + 1)
                w1_transpose(ITEM_B)
                l1_piece(0, 1)

            @block.vector
            def _(dve):
                def split_x(g):
                    for j in range(PAIRS):
                        dve.wait_ge(xhi_d, g * PAIRS + (j + 1))
                        pair = slice(2 * j, 2 * j + 2)
                        nc.vector.tensor_tensor(xT_lo[:, pair, :].rearrange("p k t -> p (k t)"), ps[:, j, :],
                                                xT_hi[:, pair, :].bitcast(F32).rearrange("p k t -> p (k t)"),
                                                ALU.subtract).then_inc(xlo_d, 1)

                def own_h(g):
                    dve.wait_ge(h_mm, g + 1)
                    nc.vector.tensor_tensor(h_own[:], ps[:, HBANK, 0:GT].rearrange("p (b s) -> p b s", b=GB),
                                            own[:].to_broadcast([P, GB, SEQ]), ALU.mult).then_inc(h_own_d, 1)

                def low_h(g):
                    dve.wait_ge(h_hi_d, g + 1)
                    nc.vector.tensor_tensor(h_lo[:], h_own[:].rearrange("p b s -> p (b s)"), h_hi[:].bitcast(F32),
                                            ALU.subtract).then_inc(h_lo_d, 1)

                def add(g, a, b):
                    add_q(g, L0_QG, L0_N0, range(a, b), 0)

                def w0_low(n):
                    prep0.low(n, PAIR0[n], AW + n * P)

                split_x(0)
                for n in range(3):
                    w0_low(n)
                dve.wait_ge(consts_ld, 64)
                nc.vector.tensor_tensor(coef[:], scale_bc, wscale_bc, ALU.mult).then_inc(dve_s, 1)
                half = P // 2
                nc.vector.tensor_copy(lang_tt[0:half, :, 0], lang_bc[0:half, 0::2]).then_inc(dve_s, 1)
                nc.vector.tensor_copy(lang_tt[half:P, :, 0], lang_bc[half:P, 1::2]).then_inc(dve_s, 1)
                dve.wait_ge(len_d, 1)
                nc.vector.tensor_tensor(len_f, len_f, scale_bc, ALU.mult).then_inc(dve_s, 1)
                dve.wait_ge(dve_s, 4)
                nc.vector.reduce_sum(s0[:], len_f, AX_X).then_inc(dve_s, 1)
                low_A(dve, 0)
                w0_low(3)
                dve.wait_ge(cst, 7)
                dve.wait_ge(dve_s, 5)
                own_h(0)
                nc.vector.tensor_tensor(lang_bias[:], lang_tt[:].to_broadcast([P, TT, NE]),
                                        iota8[:].rearrange("p (a e) -> p a e", a=1).to_broadcast([P, TT, NE]),
                                        ALU.is_equal).then_inc(dve_s, 1)
                low_h(0)
                dve.wait_ge(dve_s, 6)
                nc.vector.tensor_scalar(lang_bias[:], lang_bias[:], LANG_BIAS, None, ALU.mult).then_inc(dve_s, 1)
                w0_low(4)
                w0_low(5)
                dve.wait_ge(w3_ld, 16)
                for b in range(HB):
                    nc.vector.tensor_scalar(w3_sum[:, b, :], w3_sum[:, b, :], s0[:, 0:1], None, ALU.add)\
                      .then_inc(w3_s0, 1)
                w0_low(6)
                dve.wait_ge(w3_s0, HB)
                add(0, RING, RING + 1)
                w0_low(7)
                add(0, RING + 1, 10)
                split_x(1)
                add(0, 10, L0_QG)
                with dve.Fori(1, LG) as g:
                    add(g, 0, 2)
                    own_h(g)
                    add(g, 2, 3)
                    low_h(g)
                    add(g, 3, 10)
                    split_x(g + 1)
                    add(g, 10, L0_QG)

                def w1_low(i):
                    if i == ITEM_R:
                        prep1.low(i, PAIR1[i], ER, NE)
                    elif i == ITEM_B:
                        dve.wait_ge(prep1.hi, i + 1)
                        perm = "q (p j) -> q j p"
                        nc.vector.scalar_tensor_tensor(
                            out=b1_lo[:].rearrange(perm, j=KT), in0=tiles(2 * PAIR1[i]), scalar=SCALING,
                            in1=b1_hi[:].bitcast(F32).rearrange(perm, j=KT),
                            op0=ALU.mult, op1=ALU.subtract).then_inc(prep1.lo, 1)
                    else:
                        prep1.low(i, PAIR1[i], 0 if i == 0 else AW + SEQ1[i] * P)

                add(LG, 0, ADDS1[0])
                own_h(LG)
                low_h(LG)
                added = ADDS1[0]
                for i in range(KT):
                    w1_low(i)
                    if i == KT - 1:
                        split_x1_lo(dve, 0, 0)
                        w1_low(ITEM_R)
                    add(LG, added, added + ADDS1[i + 1])
                    added += ADDS1[i + 1]
                add_q(0, 2 * L1_QT, L0_Q, range(TAIL_Q), 0)
                gating(0, 0, lambda j: None)
                w1_low(ITEM_R + 1)
                w1_low(ITEM_B)

        x3_hi, x3_lo = x1_hi, x1_lo
        x3_hi_d, x3_lo_d = sem("x3_hi_d"), sem("x3_lo_d")
        prep3 = Prep("w3", stage, RING)
        PAIR3 = (0, 0, 1, 2)
        PER, N0 = 2 * L3_QT, L0_Q + TT * L1_QT

        def split_x3_hi(it, d):
            nc.scalar.activation(x3_hi[:, d, :, :], act[:, :, ds(it * 2 * P + d * P, P)], ACT.Copy)\
              .then_inc(x3_hi_d, 1)

        def split_x3_lo(eng, it, d):
            eng.tensor_tensor(x3_lo[:, d, :, :], act[:, :, ds(it * 2 * P + d * P, P)],
                              x3_hi[:, d, :, :].bitcast(F32), ALU.subtract).then_inc(x3_lo_d, 1)

        def l3_product(d, c0, c1, ks=range(KT)):
            half = c0 // NB * NB
            for k in ks:
                for n, (a, b) in enumerate(((x3_hi, w_hi), (x3_lo, w_hi), (x3_hi, w_lo))):
                    last = nc.tensor.matmul(ps[:, d, c0 - half:c1 - half], a[:, d, k, :], b[:, k, AW + c0:AW + c1],
                                            start=(k == 0 and n == 0), stop=(k == KT - 1 and n == 2))
            return last

        with ExitStack() as l1:
            sc_col = sb("sc_col", [NQ, 2])
            sc_ld = sem("sc_ld")
            w2_bd = sb("w2_bd", [P, 2, P], F32, l1)
            bias_bc = sb("bias_bc", [P, 2, 1, P], F32, l1)
            hg_hi = sb("hg_hi", [P, P], F32R, l1)
            hg_lo = sb("hg_lo", [P, P], F32R, l1)
            OUT2 = 6
            hgt, y1_mm, l2_mm = (sem(n) for n in ("hgt", "y1_mm", "l2_mm"))
            hg_hi_d, hg_lo_d = sem("hg_hi_d"), sem("hg_lo_d")
            w2_zero, w2_ld = sem("w2_zero"), [sem(f"w2_ld{d}") for d in range(2)]
            w2_d = sem("w2_d")
            block = l1.enter_context(nc.Block())

            @block.sync
            def _(sp):
                per, n0 = 2 * L1_QT, L0_Q
                last = TT // 2 - 1
                sp.dma_start(sc_col[:, 0:1], scale.rearrange("(n a) -> n a", a=1)).then_inc(sc_ld, 16)
                sp.dma_start(sc_col[:, 1:2], bscale.rearrange("(n a) -> n a", a=1)).then_inc(sc_ld, 16)
                for it in range(L1_UP - 1):
                    stream_q(sp, it, per, n0, range(0 if it else TAIL_Q, per), 0)
                stream_q(sp, L1_UP - 1, per, n0, range(per - RING), 0)
                for b in range(HB):
                    sp.wait_ge(sum_done, UP_Q + b + 1)
                    sp.dma_start(w3_upper[b * P:(b + 1) * P, :], w3_sum[:, b, :]).then_inc(up_st[b], 16)
                    stream_q(sp, L1_UP - 1, per, n0, [per - RING + b], 1)
                with sp.Fori(L1_UP, last) as it:
                    stream_q(sp, it, per, n0, range(per), 1)
                stream_q(sp, last, per, n0, range(per - RING), 1)
                for b in range(HB):
                    sp.wait_ge(up_st[b], 16)
                    sp.wait_ge(sum_done, L0_Q + TT * L1_QT + b + 1)
                    prep3.load(sp, b, w3_upper[b * P:(b + 1) * P, :])
                for b in range(HB):
                    sp.wait_ge(prep3.tp, b + 1)
                    load_q(sp, b, (N0 - UP_Q) // RING, 1)

            @block.gpsimd
            def _(pool):
                def load(it, d):
                    for c in range(2):
                        s = pool.value_load(subj_row[0:1, ds(it * 4 + (2 * d + c), 1)], min_val=0,
                                            max_val=w2.shape[0] - 1)
                        part = slice(c * SEQ, (c + 1) * SEQ)
                        pool.dma_start(w2_bd[part, d, part], w2[ds(s, 1), :, :].rearrange("a c n -> (a c) n"))\
                            .then_inc(w2_ld[d], 16)
                        pool.dma_start(bias_bc[:, d, 0, part],
                                       bias2[ds(s, 1), :, :].rearrange("a b n -> (a b) n").to_broadcast([P, SEQ]))\
                            .then_inc(w2_ld[d], 16)

                def tile(it, d):
                    pool.wait_ge(w2_ld[d], it * 64 + 64)
                    nc.gpsimd.tensor_tensor(w2_bd[:, d, :], w2_bd[:, d, :], ident[:], ALU.add).then_inc(w2_d, 1)

                def reload(it, d):
                    pool.wait_ge(x3_out, it * 2 + d)
                    load(it, d)

                nc.gpsimd.memset(w2_bd[:], 0.0).then_inc(w2_zero, 1)
                pool.wait_ge(w2_zero, 1)
                split_x1_lo(pool, 0, 1)
                load(0, 0)
                load(0, 1)
                tile(0, 0)
                tile(0, 1)
                split_x1_lo(pool, 1, 0)
                last = TT // 2 - 1
                with pool.Fori(1, last) as it:
                    reload(it, 0)
                    split_x1_lo(pool, it, 1)
                    tile(it, 0)
                    reload(it, 1)
                    split_x1_lo(pool, it + 1, 0)
                    tile(it, 1)
                reload(last, 0)
                split_x1_lo(pool, last, 1)
                tile(last, 0)
                reload(last, 1)
                tile(last, 1)
                pool.wait_ge(x3_hi_d, 1)
                split_x3_lo(pool, 0, 0)
                for b in range(HB):
                    prep3.add_identity(pool, b, b)

            @block.scalar
            def _(act_e):
                def gated_h(it, d):
                    act_e.wait_ge(hgt, it * 2 + (d + 1))
                    nc.scalar.activation(hg_hi[:], ps[:, OUT2, 0:P], ACT.Copy).then_inc(hg_hi_d, 1)

                def out_x2(it, d):
                    act_e.wait_ge(y1_mm, it * 2 + (d + 1))
                    for i, (c0, c1, f) in enumerate(PIECES):
                        piece = nc.scalar.activation(x2[:, f - AW:c1 - AW], ps[:, 3 * d + i, f - c0:c1 - c0], ACT.Copy)
                    piece.then_inc(x2_d, 1)

                def tile(it, d, nxt):
                    split_x1_hi(*nxt)
                    if not (isinstance(it, int) and it == 0 and d == 0):
                        exp_gap(it, d)
                    gated_h(it, d)
                    out_x2(it, d)

                tile(0, 0, (0, 1))
                tile(0, 1, (1, 0))
                with act_e.Fori(1, TT // 2 - 1) as it:
                    tile(it, 0, (it, 1))
                    tile(it, 1, (it + 1, 0))
                tile(TT // 2 - 1, 0, (TT // 2 - 1, 1))
                last = TT // 2 - 1
                act_e.wait_ge(base_mm, TT)
                act_e.wait_ge(x3_out, 2)
                split_x3_hi(0, 0)
                exp_gap(last, 1)
                gated_h(last, 1)
                prep3.high(0, PAIR3[0], AW)
                out_x2(last, 1)
                for b in range(1, HB):
                    prep3.high(b, PAIR3[b], AW + b * P)

            @block.tensor
            def _(pe):
                def l2(it, d):
                    n1 = d + 1
                    pe.wait_ge(x2_d, it * 2 + (n1 + 2))
                    pe.wait_ge(w2_d, it * 2 + n1)
                    pe.wait_ge(x3_out, it * 2 + n1)
                    for k in range(KT):
                        cols = slice(k * P, (k + 1) * P)
                        last = nc.tensor.matmul(banks(OUT2)[:, cols], x2[:, cols], w2_bd[:, d, :],
                                                start=True, stop=True)
                    last.then_inc(l2_mm, 1)

                def tile(it, d, prev, final=False):
                    n1 = d + 1
                    first_tile = isinstance(it, int) and it == 0 and d == 0
                    if not first_tile:
                        pe.wait_ge(x1_lo_d, it * 2 + n1)
                        pe.wait_ge(x2_d, it * 2 + n1)
                        l1_piece(d, 0).then_inc(h1_mm, 1)
                        l1_piece(d, 1)
                    if prev:
                        l2(*prev)
                    l1_piece(d, 2, range(6))
                    pe.wait_ge(gs, it * (2 * GS) + (d + 1) * GS)
                    pe.wait_ge(x3_out, it * 2 + n1)
                    nc.tensor.transpose(ps[:, OUT2, 0:P], hg, ident[:]).then_inc(hgt, 1)
                    last = l1_piece(d, 2, range(6, KT))
                    last.then_inc(base_mm, 1)
                    if final:
                        pe.wait_ge(prep3.ident, 1)
                        prep3.transpose(0, PAIR3[0])
                    pe.wait_ge(hg_lo_d, it * 2 + n1)
                    for i, (c0, c1, f) in enumerate(PIECES):
                        for n, (a, b) in enumerate(((hg_hi, b1_hi), (hg_lo, b1_hi), (hg_hi, b1_lo))):
                            last = nc.tensor.matmul(ps[:, 3 * d + i, f - c0:c1 - c0], a[:], b[:, f - AW:c1 - AW],
                                                    start=False, stop=(n == 2), skip_group_check=(i == 0))
                    last.then_inc(y1_mm, 1)

                tile(0, 0, None)
                tile(0, 1, (0, 0))
                last = TT // 2 - 1
                with pe.Fori(1, last) as it:
                    tile(it, 0, (it - 1, 1))
                    tile(it, 1, (it, 0))
                tile(last, 0, (last - 1, 1))
                tile(last, 1, (last, 0), final=True)
                pe.wait_ge(prep3.ident, 2)
                pe.wait_ge(prep3.lo, 1)
                prep3.transpose(1, PAIR3[1])
                l2(last, 1)
                for b in (2, 3):
                    pe.wait_ge(prep3.ident, b + 1)
                    prep3.transpose(b, PAIR3[b])
                pe.wait_ge(x3_lo_d, 1)
                pe.wait_ge(prep3.lo, 2)
                l3_product(0, 0, NB // 2)

            @block.vector
            def _(dve):
                def out_x3(it, d):
                    dve.wait_ge(l2_mm, it * 2 + (d + 1))
                    nc.vector.tensor_tensor(act[:, :, ds(it * 2 * P + d * P, P)], tiles(OUT2),
                                            bias_bc[:, d, :, :].to_broadcast([P, KT, P]), ALU.add).then_inc(x3_out, 1)

                def tile(it, d, prev, half, final=False):
                    def add(a, b):
                        if isinstance(it, int) and it == L1_UP:
                            begin = [j for j in range(d * L1_QT + a, d * L1_QT + b) if j < HB]
                            for j in begin:
                                dve.wait_ge(ring_ld[j], 16 * (UP_Q // RING + 1))
                                dve.wait_ge(up_st[j], 16)
                                nc.vector.tensor_scalar(w3_sum[:, j, :], ring[:, j, :], coef[:, 0:1], None, ALU.mult)\
                                  .then_inc(sum_done, 1)
                            a += len(begin)
                        add_q(it, 2 * L1_QT, L0_Q, range(d * L1_QT + a, d * L1_QT + b), half)

                    first = isinstance(it, int) and it == 0 and d == 0
                    if first:
                        add(TAIL_Q, 5)
                    elif isinstance(it, int) and it == L1_UP and d == 0:
                        gating(it, d, lambda j: add(j, 1 + j))
                    else:
                        add(0, 3)
                        gating(it, d, lambda j: add(3 + j, 4 + j))
                    if prev:
                        out_x3(*prev)
                    if not first:
                        add(2 if isinstance(it, int) and it == L1_UP and d == 0 else 5, 6)
                    dve.wait_ge(hg_hi_d, it * 2 + (d + 1))
                    nc.vector.tensor_tensor(hg_lo[:], ps[:, OUT2, 0:P], hg_hi[:].bitcast(F32), ALU.subtract)\
                      .then_inc(hg_lo_d, 1)
                    add(5 if first else 6, 8)
                    if final:
                        prep3.low(0, PAIR3[0], AW)

                def pair(it, half):
                    tile(it, 0, (it - 1, 1), half)
                    tile(it, 1, (it, 0), half)

                tile(0, 0, None, 0)
                tile(0, 1, (0, 0), 0)
                with dve.Fori(1, L1_UP) as it:
                    pair(it, 0)
                pair(L1_UP, 1)
                last = TT // 2 - 1
                with dve.Fori(L1_UP + 1, last) as it:
                    pair(it, 1)
                tile(last, 0, (last - 1, 1), 1)
                tile(last, 1, (last, 0), 1, final=True)
                for b in (1, 2):
                    prep3.low(b, PAIR3[b], AW + b * P)
                out_x3(last, 1)
                prep3.low(3, PAIR3[3], AW + 3 * P)

        with ExitStack() as l3:
            b3_bc = B_raw
            y_sb = sb("y_sb", [P, 2, NB], F32, l3)
            low_rows = rows_in
            bq_i = low_rows[0:NQ, 0, :].bitcast(I32)
            bq_f = y_sb[0:NQ, :, :].rearrange("p a n -> p (a n)")
            cb = sb("cb", [NQ, 1], F32, l3)
            cb_bc = sb("cb_bc", [NQ, P], F32, l3)
            ones = sb("ones", [NQ, P], F32, l3)
            b3_ld, b3_s, b3_mm, bq_cv, b3_out = (sem(n) for n in ("b3_ld", "b3_s", "b3_mm", "bq_cv", "b3_out"))
            bq_ld = sem("bq_ld")
            y3_mm = sem("y3_mm")
            y3_st = [sem(f"y3_st{d}") for d in range(2)]
            low_ld, low_w = sem("low_ld"), sem("low_w")
            low_id, low_tp, low_hi, low_lo = (sem(n) for n in ("low_id", "low_tp", "low_hi", "low_lo"))
            ITS = TT // 2
            SPLIT_K = 4
            LOW_BANKS = (2, 4, 6, 2)
            block = l3.enter_context(nc.Block())

            @block.sync
            def _(sp):
                def store(it, d, half):
                    sp.wait_ge(y3_out, it * 2 + (half * TT + d + 3))
                    sp.dma_start(y_rows[ds(it * 2 * P + d * P, P), half * NB:(half + 1) * NB], y_sb[:, d, :])\
                      .then_inc(y3_st[d], 16)

                sp.dma_start(bq_i, bq).then_inc(bq_ld, 16)
                sp.dma_start(b3_bc[:], row(b3).to_broadcast([P, D])).then_inc(b3_ld, 16)
                sp.wait_ge(bq_cv, 1)
                def load_low(pair):
                    r0 = HALF + pair * 2 * P
                    sp.dma_start(low_rows[:], W3[r0:r0 + 2 * P, :].rearrange("(b p) n -> p b n", p=P))\
                      .then_inc(low_ld, 16)

                def pair_of_tiles(it):
                    for d in range(2):
                        stream_q(sp, it, PER, N0, range(d * L3_QT, (d + 1) * L3_QT), 1)
                        store(it, d, 0)

                load_low(0)
                pair_of_tiles(0)
                sp.wait_ge(low_w, 2)
                load_low(1)
                with sp.Fori(1, ITS - 1) as it:
                    pair_of_tiles(it)
                for d in range(2):
                    store(ITS - 1, d, 0)
                with sp.Fori(0, ITS) as it:
                    for d in range(2):
                        store(it, d, 1)
                for d in range(2):
                    sp.wait_ge(y3_st[d], 2 * 16 * ITS)

            @block.gpsimd
            def _(pool):
                for b in range(HB):
                    pool.wait_ge(sum_done, 2 * UP_Q + RING - HB + b + 1)
                    diag = w3_sum[:, b, (HB + b) * P:(HB + b + 1) * P]
                    nc.gpsimd.tensor_tensor(diag, diag, ident[:], ALU.add).then_inc(low_id, 1)

            @block.scalar
            def _(act_e):
                def split(it, d, half):
                    if not (isinstance(it, int) and it == 0 and half == 0):
                        act_e.wait_ge(y3_mm, it * 2 + (half * TT + d - 1))
                    split_x3_hi(it, d)

                split(0, 1, 0)
                act_e.wait_ge(bq_ld, 16)
                nc.scalar.activation(bq_f, bq_i, ACT.Copy).then_inc(bq_cv, 1)
                with act_e.Fori(1, ITS) as it:
                    for d in range(2):
                        split(it, d, 0)
                split(0, 0, 1)
                for b in range(HB):
                    act_e.wait_ge(low_tp, b + 1)
                    o = AW + (HB + b) * P
                    nc.scalar.activation(w_hi[:, :, o:o + P], tiles(LOW_BANKS[b]), ACT.Copy)\
                      .then_inc(low_hi, 1)
                split(0, 1, 1)
                with act_e.Fori(1, ITS) as it:
                    for d in range(2):
                        split(it, d, 1)

            @block.tensor
            def _(pe):
                def tile(it, d, half):
                    pe.wait_ge(x3_lo_d, it * 2 + (half * TT + d + 1))
                    pe.wait_ge(y3_out, it * 2 + (half * TT + d + 1))
                    l3_product(d, half * NB, (half + 1) * NB).then_inc(y3_mm, 1)

                l3_product(0, NB // 2, NB).then_inc(y3_mm, 1)
                pe.wait_ge(x3_lo_d, 2)
                l3_product(1, 0, NB, range(SPLIT_K))
                pe.wait_ge(b3_s, 3)
                pe.wait_ge(bq_cv, 1)
                for half in range(2):
                    cols = slice(half * NB, (half + 1) * NB)
                    last = nc.tensor.matmul(ps[:, 2 + half, :], cb_bc[:], bq_f[:, cols], start=True, stop=True)
                last.then_inc(b3_mm, 1)
                l3_product(1, 0, NB, range(SPLIT_K, KT)).then_inc(y3_mm, 1)
                with pe.Fori(1, ITS - 1) as it:
                    tile(it, 0, 0)
                    tile(it, 1, 0)
                tile(ITS - 1, 0, 0)
                pe.wait_ge(x3_lo_d, TT)
                pe.wait_ge(y3_out, TT)
                l3_product(1, 0, NB, range(SPLIT_K))
                for b in range(HB):
                    pe.wait_ge(low_id, b + 1)
                    if b == 3:
                        pe.wait_ge(low_lo, 1)
                    for k in range(KT):
                        last = nc.tensor.transpose(banks(LOW_BANKS[b])[:, k * P:(k + 1) * P],
                                                   w3_sum[:, b, k * P:(k + 1) * P], ident[:])
                    last.then_inc(low_tp, 1)
                l3_product(1, 0, NB, range(SPLIT_K, KT)).then_inc(y3_mm, 1)
                pe.wait_ge(low_lo, HB)
                with pe.Fori(0, ITS) as it:
                    tile(it, 0, 1)
                    tile(it, 1, 1)

            @block.vector
            def _(dve):
                def split(it, d, half):
                    dve.wait_ge(x3_hi_d, it * 2 + (half * TT + d + 1))
                    split_x3_lo(dve, it, d)

                def out(it, d, half):
                    dve.wait_ge(y3_mm, it * 2 + (half * TT + d + 1))
                    if not (isinstance(it, int) and it == 0 and half == 0):
                        dve.wait_ge(y3_st[d], it * 16 + 16 * half * ITS)
                    nc.vector.tensor_tensor(y_sb[:, d, :], ps[:, d, :], b3_bc[:, half * NB:(half + 1) * NB],
                                            ALU.add).then_inc(y3_out, 1)

                def tile(it, d, nxt, low=None, qs=None):
                    split(*nxt)
                    if low is not None:
                        dve.wait_ge(low_ld, 16 * (low // 2 + 1))
                        dve.wait_ge(sum_done, N0 + RING + it * PER + d * L3_QT)
                        nc.vector.scalar_tensor_tensor(
                            out=w3_sum[:, low, :], in0=low_rows[:, low % 2, :], scalar=s0[:, 0:1],
                            in1=w3_sum[:, low, :], op0=ALU.add, op1=ALU.add).then_inc(low_w, 1)
                        dve.wait_ge(low_w, low + 1)
                    add_q(it, PER, N0, range(d * L3_QT, (d + 1) * L3_QT) if qs is None else qs, 1)
                    out(it, d, 0)

                nc.vector.memset(ones[:], 1.0).then_inc(b3_s, 1)
                split(0, 1, 0)
                dve.wait_ge(sc_ld, 32)
                nc.vector.tensor_tensor(cb[:], sc_col[:, 0:1], sc_col[:, 1:2], ALU.mult).then_inc(b3_s, 1)
                dve.wait_ge(b3_s, 2)
                nc.vector.tensor_scalar(cb_bc[:], ones[:], cb[:, 0:1], None, ALU.mult).then_inc(b3_s, 1)
                LAST = ITS - 1
                add_q(0, PER, N0, range(L3_QT), 1)
                dve.wait_ge(b3_ld, 16)
                dve.wait_ge(b3_mm, 1)
                nc.vector.scalar_tensor_tensor(out=b3_bc[:], in0=banks(2), scalar=s0[:, 0:1], in1=b3_bc[:],
                                               op0=ALU.add, op1=ALU.add).then_inc(b3_out, 1)
                dve.wait_ge(b3_out, 1)
                out(0, 0, 0)
                tile(0, 1, (1, 0, 0), low=0)
                tile(1, 0, (1, 1, 0), low=1)
                tile(1, 1, (2, 0, 0))
                tile(2, 0, (2, 1, 0), low=2)
                tile(2, 1, (3, 0, 0), low=3)
                with dve.Fori(3, LAST) as it:
                    tile(it, 0, (it, 1, 0))
                    tile(it, 1, (it + 1, 0, 0))
                tile(LAST, 0, (LAST, 1, 0), qs=range(PER))
                split(0, 0, 1)
                for b in range(HB):
                    dve.wait_ge(low_hi, b + 1)
                    o = slice(AW + (HB + b) * P, AW + (HB + b + 1) * P)
                    nc.vector.tensor_tensor(w_lo[:, :, o], tiles(LOW_BANKS[b]), w_hi[:, :, o].bitcast(F32),
                                            ALU.subtract).then_inc(low_lo, 1)
                out(LAST, 1, 0)
                split(0, 1, 1)
                out(0, 0, 1)
                with dve.Fori(1, ITS) as it:
                    split(it, 0, 1)
                    out(it - 1, 1, 1)
                    split(it, 1, 1)
                    out(it, 0, 1)
                out(ITS - 1, 1, 1)


_INS = ["x", "condB_scale", "condB_wscale", "condB_bscale", "_lenS", "itok_B_0_23", "itok_B_0_7",
        "itok_B_0_31", "itok_Bx4096x4096_0_255", "itok_Bx4096_0_255", "L0_cond_W", "L0_cond_b",
        "L0_cond_lora_As", "L0_cond_lora_Bs", "L1_cond_W", "L1_cond_Wr", "L1_cond_A", "L1_cond_B",
        "L2_cond_weights", "L2_cond_biases", "L3_cond_weight", "L3_cond_bias"]


def kernel(**inputs):
    import numpy as np
    import concourse.bacc as bacc
    from concourse.bass_utils import run_bass_kernel_spmd

    nc = bacc.Bacc("TRN2", target_bir_lowering=False, num_devices=1)
    arrays, args = {}, []
    for name in _INS:
        a = np.ascontiguousarray(inputs[name])
        arrays[f"in_{name}"] = a
        args.append(nc.dram_tensor(f"in_{name}", a.shape, mybir.dt.from_np(a.dtype), kind="ExternalInput").ap())
    args.append(nc.dram_tensor("out", (BATCH, SEQ, D), F32, kind="ExternalOutput").ap())
    program(nc, *args)
    return run_bass_kernel_spmd(nc, [arrays], core_ids=[0]).results[0]["out"]
```
